# Optimizing a Trainium2 kernel written in Bass

```python
import numpy as np
import jax
import jax.numpy as jnp

def _softmax(x, axis=-1):
    return jax.nn.softmax(x, axis=axis)

def _gelu(x):
    return jax.nn.gelu(x, approximate=True)

def _silu(x):
    return jax.nn.silu(x)

def _sigmoid(x):
    return jax.nn.sigmoid(x)

def _layernorm(x, axis=-1, eps=1e-05):
    m = jnp.mean(x, axis=axis, keepdims=True)
    v = jnp.var(x, axis=axis, keepdims=True)
    return (x - m) / jnp.sqrt(v + eps)

def _scatter_add(tgt, idx, src, axis=0):
    return tgt.at[idx].add(src)

def _segment_sum(src, seg, n):
    return jax.ops.segment_sum(src, seg, n)
kernel_name = 'mk_conv_preact_d2_conv_nchw64_r2_a839ab'

def setup_inputs(seed: int=0):
    np.random.seed(seed)
    _w = jnp.asarray

    def _rec_inputs():
        import jax
        import jax.numpy as jnp
        _gk = jax.random.key(seed)
        x = -0.0003957 + 1 * jax.random.normal(jax.random.fold_in(_gk, 1), (32, 32, 56, 56), jnp.float32)
        return x
    x = _rec_inputs()

    def _L0_conv_setup():
        import jax, jax.numpy as jnp
        import numpy as np
        K = 3
        STRIDE = 1
        PAD = 1
        C_IN = 32
        C_OUT = 32
        OUT_H = 56
        OUT_W = 56
        IN_DIM = C_IN * K * K
        POSITIONS = OUT_H * OUT_W
        BATCH = 32

        def _unfold(x, k, stride, padding):
            xp = jnp.pad(x, ((0, 0), (0, 0), (padding, padding), (padding, padding)))
            B, C, Hp, Wp = xp.shape
            oh = (Hp - k) // stride + 1
            ow = (Wp - k) // stride + 1
            tiles = [xp[:, :, i:i + stride * oh:stride, j:j + stride * ow:stride] for i in range(k) for j in range(k)]
            patches = jnp.stack(tiles, axis=2)
            return patches.reshape(B, C * k * k, oh * ow)
        key = jax.random.key(seed)
        kx, kw = jax.random.split(key)
        x = jax.random.normal(kx, (BATCH, C_IN, OUT_H, OUT_W), dtype=jnp.float32)
        std = float(np.sqrt(2.0 / IN_DIM))
        weight = jax.random.normal(kw, (C_OUT, POSITIONS, IN_DIM), dtype=jnp.float32) * std
        bias = jnp.zeros((C_OUT, POSITIONS), dtype=jnp.float32)
        return {'x': x, 'weight': weight, 'bias': bias}
    _L0_conv_all = _L0_conv_setup()
    _L0_conv_in = {k: v for k, v in _L0_conv_all.items() if k in ('weight', 'bias')}
    del _L0_conv_all

    def _L1_conv_setup():
        import jax, jax.numpy as jnp
        import numpy as np
        B, C, H, W, K, OUT = (8, 32, 56, 56, 16, 32)
        BN_EPS = 1e-05

        def _pairwise_distance(p):
            inner = -2.0 * jnp.einsum('bnc,bmc->bnm', p, p)
            sq = jnp.sum(p * p, axis=-1, keepdims=True)
            return sq + inner + jnp.swapaxes(sq, 1, 2)
        key = jax.random.key(seed)
        ks = jax.random.split(key, 5)
        return {'x': jax.random.normal(ks[0], (B, C, H, W), jnp.float32), 'W_emb': jax.random.normal(ks[1], (C, C), jnp.float32) * 0.05, 'b_emb': jnp.zeros((C,), jnp.float32), 'W_att': jax.random.normal(ks[2], (2 * C, 1), jnp.float32) * 0.05, 'b_att': jnp.zeros((1,), jnp.float32), 'W_conv': jax.random.normal(ks[3], (2 * C, OUT), jnp.float32) * 0.05, 'b_conv': jnp.zeros((OUT,), jnp.float32), 'gamma': jnp.ones((OUT,), jnp.float32), 'beta': jnp.zeros((OUT,), jnp.float32)}
    _L1_conv_all = _L1_conv_setup()
    _L1_conv_in = {k: v for k, v in _L1_conv_all.items() if k in ('W_emb', 'b_emb', 'W_att', 'b_att', 'W_conv', 'b_conv', 'gamma', 'beta')}
    del _L1_conv_all
    return {'x': x, 'L0_conv_weight': _L0_conv_in['weight'], 'L0_conv_bias': _L0_conv_in['bias'], 'L1_conv_W_emb': _L1_conv_in['W_emb'], 'L1_conv_b_emb': _L1_conv_in['b_emb'], 'L1_conv_W_att': _L1_conv_in['W_att'], 'L1_conv_b_att': _L1_conv_in['b_att'], 'L1_conv_W_conv': _L1_conv_in['W_conv'], 'L1_conv_b_conv': _L1_conv_in['b_conv'], 'L1_conv_gamma': _L1_conv_in['gamma'], 'L1_conv_beta': _L1_conv_in['beta']}

def reference(x, L0_conv_weight, L0_conv_bias, L1_conv_W_emb, L1_conv_b_emb, L1_conv_W_att, L1_conv_b_att, L1_conv_W_conv, L1_conv_b_conv, L1_conv_gamma, L1_conv_beta):
    import jax
    import jax.numpy as jnp

    def _L0_conv_ref(x, weight, bias):
        import jax, jax.numpy as jnp
        import numpy as np
        K = 3
        STRIDE = 1
        PAD = 1
        C_IN = 32
        C_OUT = 32
        OUT_H = 56
        OUT_W = 56
        IN_DIM = C_IN * K * K
        POSITIONS = OUT_H * OUT_W
        BATCH = 32

        def _unfold(x, k, stride, padding):
            xp = jnp.pad(x, ((0, 0), (0, 0), (padding, padding), (padding, padding)))
            B, C, Hp, Wp = xp.shape
            oh = (Hp - k) // stride + 1
            ow = (Wp - k) // stride + 1
            tiles = [xp[:, :, i:i + stride * oh:stride, j:j + stride * ow:stride] for i in range(k) for j in range(k)]
            patches = jnp.stack(tiles, axis=2)
            return patches.reshape(B, C * k * k, oh * ow)
        B = x.shape[0]
        patches = _unfold(x, K, STRIDE, PAD)
        patches = patches.transpose(0, 2, 1)
        out = jnp.einsum('bpi,opi->bop', patches, weight)
        out = out + bias[None, :, :]
        return out.reshape(B, C_OUT, OUT_H, OUT_W)

    def _L1_conv_ref(x, W_emb, b_emb, W_att, b_att, W_conv, b_conv, gamma, beta):
        import jax, jax.numpy as jnp
        import numpy as np
        B, C, H, W, K, OUT = (8, 32, 56, 56, 16, 32)
        BN_EPS = 1e-05

        def _pairwise_distance(p):
            inner = -2.0 * jnp.einsum('bnc,bmc->bnm', p, p)
            sq = jnp.sum(p * p, axis=-1, keepdims=True)
            return sq + inner + jnp.swapaxes(sq, 1, 2)
        b, c, h, w = x.shape
        n = h * w
        pts = x.reshape(b, c, n).transpose(0, 2, 1)
        p = jax.lax.stop_gradient(pts)
        p = p / jnp.maximum(jnp.linalg.norm(p, axis=1, keepdims=True), 1e-12)
        dist = _pairwise_distance(p)
        _, nn_idx = jax.lax.top_k(-dist, K)
        bidx = jnp.arange(b)[:, None, None]
        nbr = pts[bidx, nn_idx]
        e = pts @ W_emb + b_emb
        e_n = nbr @ W_emb + b_emb
        cat = jnp.concatenate([jnp.broadcast_to(e[:, :, None, :], e_n.shape), e_n], axis=-1)
        logits = jax.nn.leaky_relu(cat @ W_att + b_att, negative_slope=0.1)
        attn = jax.nn.softmax(logits, axis=2)
        agg = jnp.sum(nbr * attn, axis=2)
        hfeat = jnp.concatenate([pts, agg], axis=-1)
        y = hfeat @ W_conv + b_conv
        mu = jnp.mean(y, axis=(0, 1))
        var = jnp.var(y, axis=(0, 1))
        y = (y - mu) / jnp.sqrt(var + BN_EPS) * gamma + beta
        y = jax.nn.relu(y)
        y = y + pts
        return y.transpose(0, 2, 1).reshape(b, -1, h, w)

    def _gn(v, G=32, eps=1e-05):
        B_, C_, H_, W_ = v.shape
        g = v.reshape(B_, G, C_ // G, H_, W_)
        m = jnp.mean(g, axis=(2, 3, 4), keepdims=True)
        s = jnp.var(g, axis=(2, 3, 4), keepdims=True)
        return ((g - m) / jnp.sqrt(s + eps)).reshape(v.shape)

    def _ln_c(v, eps=1e-06):
        m = jnp.mean(v, axis=1, keepdims=True)
        s = jnp.var(v, axis=1, keepdims=True)
        return (v - m) / jnp.sqrt(s + eps)

    def _ln_t(v, eps=1e-05):
        m = jnp.mean(v, axis=-1, keepdims=True)
        s = jnp.var(v, axis=-1, keepdims=True)
        return (v - m) / jnp.sqrt(s + eps)

    def _to_tokens(v):
        B_, C_, H_, W_ = v.shape
        return v.reshape(B_, C_, H_ * W_).transpose(0, 2, 1)

    def _from_tokens(t, like):
        B_, C_, H_, W_ = like.shape
        return t.transpose(0, 2, 1).reshape(B_, C_, H_, W_)
    x = x + _L0_conv_ref(_gn(x), L0_conv_weight, L0_conv_bias)
    x = x + _L1_conv_ref(_gn(x), L1_conv_W_emb, L1_conv_b_emb, L1_conv_W_att, L1_conv_b_att, L1_conv_W_conv, L1_conv_b_conv, L1_conv_gamma, L1_conv_beta)
    return x

_drawn_inputs = setup_inputs


def setup_inputs(seed=0):
    import zlib

    import numpy as np

    out = dict(_drawn_inputs(seed))
    spreads = {'L0_conv_bias': (0.0, 0.1),
     'L1_conv_b_emb': (0.0, 0.8),
     'L1_conv_b_conv': (0.0, 0.8),
     'L1_conv_gamma': (1.0, 0.2),
     'L1_conv_beta': (0.0, 0.286)}
    factors = {'L1_conv_W_emb': 8.0, 'L1_conv_W_att': 8.0}
    for name, (base, spread) in spreads.items():
        noise = np.random.default_rng([zlib.crc32(name.encode()), seed]).standard_normal(out[name].shape)
        drawn = base * np.exp(spread * noise) if base else spread * noise
        out[name] = jnp.asarray(drawn.astype(out[name].dtype))
    for name, factor in factors.items():
        out[name] = (out[name] * factor).astype(out[name].dtype)
    return out
```

```python
from contextlib import ExitStack

import concourse.bass as bass
from concourse import mybir

FP32 = mybir.dt.float32
U32 = mybir.dt.uint32
ALU = mybir.AluOpType
ACT = mybir.ActivationFunctionType
AX = mybir.AxisListType

BATCH, C, H, W = 32, 32, 56, 56
N = H * W
K = 3
IN_DIM = C * K * K
NEIGHBOURS = 16
P = 128
PER = P // C
GROUPS = BATCH // PER
HP, WP = H + 2, W + 2
EPS = 1e-5
CH = 448
NCH = N // CH
QN = N // PER
QH = H // PER
ROWLEN = C + 2
TCOLS = 112
TSTEP = N // TCOLS


def gate(engine, sem, value, passed):
    engine.wait_ge(sem, value)
    engine.sem_inc(passed, 1)


def normalise_input(nc, x, xg):
    x_rows = x.rearrange("b c h w -> (b c) (h w)")
    with ExitStack() as stack:
        enter = stack.enter_context
        x_in = enter(nc.sbuf_tensor("x_in", [P, 2, N], FP32))
        padded = enter(nc.sbuf_tensor("padded", [P, 2, H, WP], FP32))
        stats = enter(nc.sbuf_tensor("stats", [P, 2, NCH, 6], FP32))
        moments = enter(nc.sbuf_tensor("moments", [P, 2, 2], FP32))
        std = enter(nc.sbuf_tensor("std", [P, 2], FP32))
        scale = enter(nc.sbuf_tensor("scale", [P, 2], FP32))
        shift = enter(nc.sbuf_tensor("shift", [P, 2], FP32))
        eps = enter(nc.sbuf_tensor("eps", [P, 1], FP32))
        zero_row = enter(nc.sbuf_tensor("zero_row", [C, BATCH * WP], FP32))
        x_loaded0 = enter(nc.semaphore("n0_x_loaded0"))
        x_loaded1 = enter(nc.semaphore("n0_x_loaded1"))
        cleared = enter(nc.semaphore("n0_cleared"))
        chain = enter(nc.semaphore("n0_chain"))
        moments_ready = enter(nc.semaphore("n0_moments_ready"))
        std_ready = enter(nc.semaphore("n0_std_ready"))
        coef_ready = enter(nc.semaphore("n0_coef_ready"))
        normed = enter(nc.semaphore("n0_normed"))
        border_stored = enter(nc.semaphore("n0_border"))
        stored0 = enter(nc.semaphore("n0_stored0"))
        stored1 = enter(nc.semaphore("n0_stored1"))
        block = enter(nc.Block())
        x_loaded = [x_loaded0, x_loaded1]
        stored = [stored0, stored1]
        x_free_credit = 2

        @block.gpsimd
        def _(pool):
            with pool.Fori(0, GROUPS // 2) as i:
                for par in range(2):
                    g = i * 2 + par
                    pool.wait_ge(normed, g + 1)
                    pool.dma_start(x_in[:, par, :], x_rows[bass.ds(g * P, P), :]).then_inc(x_loaded[par], 16)

        @block.vector
        def _(dve):
            nc.vector.memset(padded[:], 0.0).then_inc(cleared, 1)
            nc.vector.memset(eps[:], EPS).then_inc(cleared, 1)
            nc.vector.memset(zero_row[:], 0.0).then_inc(cleared, 1)
            with dve.Fori(0, GROUPS // 2) as i:
                for par in range(2):
                    g = i * 2 + par
                    dve.wait_ge(x_loaded[par], 16 * i + 16)
                    for c in range(NCH):
                        nc.vector.bn_stats(stats[:, par, c, :], x_in[:, par, c * CH:(c + 1) * CH]).then_inc(chain, 1)
                    dve.wait_ge(chain, NCH)
                    nc.vector.bn_aggr(moments[:, par, :], stats[:, par, :, :].rearrange("p a b -> p (a b)")).then_inc(moments_ready, 1)
                    dve.wait_ge(std_ready, g + 1)
                    nc.vector.reciprocal(scale[:, par:par + 1], std[:, par:par + 1]).then_inc(chain, 1)
                    dve.wait_ge(chain, NCH + 1)
                    nc.vector.scalar_tensor_tensor(shift[:, par:par + 1], moments[:, par, 0:1], -1.0, scale[:, par:par + 1],
                                                   ALU.mult, ALU.mult).then_inc(coef_ready, 1)
                    dve.sem_clear(chain)

        @block.scalar
        def _(act):
            act.sem_inc(normed, x_free_credit)
            act.wait_ge(cleared, 3)
            with act.Fori(0, GROUPS // 2) as i:
                for par in range(2):
                    g = i * 2 + par
                    act.wait_ge(moments_ready, g + 1)
                    nc.scalar.activation(std[:, par:par + 1], moments[:, par, 1:2], ACT.Sqrt, bias=eps[:, 0:1]).then_inc(std_ready, 1)
                    act.wait_ge(coef_ready, g + 1)
                    act.wait_ge(stored[par], 16 * PER * (i + 1))
                    nc.scalar.activation(padded[:, par, :, 1:1 + W], x_in[:, par, :].rearrange("p (h w) -> p h w", w=W),
                                         ACT.Identity, bias=shift[:, par:par + 1], scale=scale[:, par:par + 1]).then_inc(normed, 1)

        @block.sync
        def _(sp):
            for par in range(2):
                sp.sem_inc(stored[par], 16 * PER)
            sp.wait_ge(cleared, 3)
            sp.dma_start(xg[:, 0, :, :].rearrange("c b w -> c (b w)"), zero_row[:, :]).then_inc(border_stored, 16)
            sp.dma_start(xg[:, HP - 1, :, :].rearrange("c b w -> c (b w)"), zero_row[:, :]).then_inc(border_stored, 16)
            with sp.Fori(0, GROUPS // 2) as i:
                for par in range(2):
                    g = i * 2 + par
                    sp.wait_ge(normed, g + 1 + x_free_credit)
                    for j in range(PER):
                        sp.dma_start(xg[:, 1:1 + H, bass.ds(g * PER + j, 1), :].rearrange("c h b w -> c h (b w)"),
                                       padded[C * j:C * (j + 1), par, :, :]).then_inc(stored[par], 16)
            sp.wait_ge(border_stored, 32)
            for par in range(2):
                sp.wait_ge(stored[par], 16 * PER * (GROUPS // 2 + 1))


def convolve(nc, weight, xg, conv):
    SLOTS = 4
    CHUNKS = W // (2 * SLOTS)
    KC = K * C
    with ExitStack() as stack:
        enter = stack.enter_context
        windows = enter(nc.sbuf_tensor("windows", [KC, 2, PER, BATCH * WP], FP32))
        w_in = enter(nc.sbuf_tensor("w_in", [P, 2, SLOTS, IN_DIM], FP32))
        w_turned = enter(nc.sbuf_tensor("w_turned", [KC, 4, K * P], FP32))
        conv_sb = enter(nc.sbuf_tensor("conv_sb", [P, BATCH, QN], FP32))
        ident = enter(nc.sbuf_tensor("ident_c", [P, P], FP32))
        w_ps = enter(nc.psum_tensor("w_ps", [P, 2, 512], FP32))
        conv_ps = enter(nc.psum_tensor("conv_ps", [P, 2, SLOTS, P], FP32))
        ident_ready = enter(nc.semaphore("c_ident"))
        win0 = enter(nc.semaphore("c_win0"))
        win1 = enter(nc.semaphore("c_win1"))
        w0 = enter(nc.semaphore("c_w0"))
        w1 = enter(nc.semaphore("c_w1"))
        turned = enter(nc.semaphore("c_turned"))
        wt_ready = enter(nc.semaphore("c_wt_ready"))
        multiplied = enter(nc.semaphore("c_multiplied"))
        copied = enter(nc.semaphore("c_copied"))
        out_stored = enter(nc.semaphore("c_out"))
        passed = enter(nc.semaphore("c_passed"))
        block = enter(nc.Block())
        win_loaded, w_loaded = [win0, win1], [w0, w1]
        xg_rows = xg.rearrange("c h b w -> c h (b w)")
        weight_rows = weight.rearrange("o p i -> o (p i)")
        TURN_FREE, WT_FREE, MUL_FREE, COPY_FREE = 2 * SLOTS, 2, 2 * W, 2

        def each_half(engine, body):
            with engine.Fori(0, QH // 2) as t:
                for r in range(2):
                    row = t * 2 + r
                    body(row, None, None, r, None)
                    with engine.Fori(0, CHUNKS) as j:
                        for u in range(2):
                            body(row, (row * CHUNKS + j) * (2 * SLOTS) + u * SLOTS, j, r, u)

        @block.sync
        def _(sp):
            def body(row, before, j, r, u):
                if u is None:
                    sp.wait_ge(multiplied, row * W + W)
                    for k in range(K):
                        sp.dma_start(windows[k:KC:K, r, :, :],
                                     xg_rows[:, bass.ds(row + k, PER, QH), :]).then_inc(win_loaded[r], 16)
                    return
                sp.wait_ge(turned, before + SLOTS)
                for q in range(PER):
                    at = (row * W + j * (2 * SLOTS) + (u * SLOTS + q * QN)) * IN_DIM
                    sp.dma_start(w_in[C * q:C * (q + 1), u, :, :].rearrange("o s i -> o (s i)"),
                                 weight_rows[:, bass.ds(at, SLOTS * IN_DIM)]).then_inc(w_loaded[u], 16)

            each_half(sp, body)
            for q in range(PER):
                sp.wait_ge(copied, QN // SLOTS + COPY_FREE)
                sp.dma_start(conv[:, :, q * QN:(q + 1) * QN].rearrange("b c n -> c b n"),
                             conv_sb[C * q:C * (q + 1), :, :]).then_inc(out_stored, 16)
            sp.wait_ge(out_stored, 16 * PER)

        @block.gpsimd
        def _(pool):
            nc.gpsimd.memset(ident[:], 0.0).then_inc(ident_ready, 1)
            pool.wait_ge(ident_ready, 1)
            nc.gpsimd.affine_select(out=ident[:], in_=ident[:], compare_op=ALU.not_equal, fill=1.0, base=0,
                                    pattern=[[-1, P]], channel_multiplier=1).then_inc(ident_ready, 1)

        @block.tensor
        def _(pe):
            pe.sem_inc(turned, TURN_FREE)
            pe.sem_inc(multiplied, MUL_FREE)
            pe.wait_ge(ident_ready, 2)

            def turn(before, s, u):
                pe.wait_ge(wt_ready, before + (s + 1))
                for k in range(K):
                    last = nc.tensor.transpose(w_ps[0:KC, s % 2, k * P:(k + 1) * P], w_in[:, u, s, k::K], ident[:])
                last.then_inc(turned, 1)

            def body(row, before, j, r, u):
                if u is None:
                    gate(pe, win_loaded[r], (row - r) * (8 * K) + 16 * K, passed)
                    return
                pe.wait_ge(w_loaded[u], (row * CHUNKS + j) * (16 * PER) + 16 * PER)
                turn(before, 0, u)
                pe.wait_ge(copied, (row * CHUNKS + j) * 2 + (u + 1))
                for s in range(SLOTS):
                    if s + 1 < SLOTS:
                        turn(before, s + 1, u)
                    pe.wait_ge(wt_ready, before + (s + 1 + WT_FREE))
                    for k in range(K):
                        x_k = windows[:, r, :, :].rearrange("p q (b w) -> p q b w", w=WP)[:, :, :, bass.ds(j * (2 * SLOTS) + (u * SLOTS + s + k), 1)]
                        last = nc.tensor.matmul(conv_ps[:, u, s, :], w_turned[:, s, k * P:(k + 1) * P], x_k,
                                                start=k == 0, stop=k == K - 1)
                    last.then_inc(multiplied, 1)

            each_half(pe, body)

        @block.scalar
        def _(act):
            act.sem_inc(wt_ready, WT_FREE)

            def body(row, before, j, r, u):
                if u is None:
                    return
                for s in range(SLOTS):
                    act.wait_ge(turned, before + (s + 1 + TURN_FREE))
                    act.wait_ge(multiplied, before + (s - SLOTS + 1 + MUL_FREE))
                    nc.scalar.activation(w_turned[:, s, :], w_ps[0:KC, s % 2, 0:K * P], ACT.Copy).then_inc(wt_ready, 1)

            each_half(act, body)

        @block.vector
        def _(dve):
            dve.sem_inc(copied, COPY_FREE)

            def body(row, before, j, r, u):
                if u is None:
                    return
                dve.wait_ge(multiplied, before + (SLOTS + MUL_FREE))
                for q in range(PER):
                    rows = slice(C * q, C * (q + 1))
                    last = nc.vector.tensor_copy(
                        conv_sb[rows, :, bass.ds(row * W + (j * (2 * SLOTS) + u * SLOTS), SLOTS)],
                        conv_ps[rows, u, :, C * q:C * q + BATCH].rearrange("p s b -> p b s"))
                last.then_inc(copied, 1)

            each_half(dve, body)


def prepare(nc, x, conv, bias, W_emb, W_att, feat, unit, base, half_sq, table):
    conv_rows, base_rows = conv.rearrange("b c n -> (b c) n"), base.rearrange("b c n -> (b c) n")
    x_rows = x.rearrange("b c h w -> (b c) (h w)")
    TBANK = 3
    TBANKS = -(-TSTEP // TBANK)
    TRING = 4
    TW = PER * ROWLEN
    STORES = 2 + 3 * PER
    with ExitStack() as stack:
        enter = stack.enter_context
        x1_sb = enter(nc.sbuf_tensor("x1_sb", [P, 2, N], FP32))
        x_sb = enter(nc.sbuf_tensor("x_sb", [P, 2, N], FP32))
        feat_sb = enter(nc.sbuf_tensor("feat_sb", [P, 2, N], FP32))
        unit_sb = enter(nc.sbuf_tensor("unit_sb", [P, 2, N], FP32))
        squares = enter(nc.sbuf_tensor("squares", [P, N], FP32))
        bias_sb = enter(nc.sbuf_tensor("bias_sb", [P, N], FP32))
        table_sb = enter(nc.sbuf_tensor("table_sb", [TCOLS, 2, PER, TSTEP, ROWLEN], FP32))
        half_sb = enter(nc.sbuf_tensor("half_sb", [PER, N], FP32))
        stats = enter(nc.sbuf_tensor("stats_p", [P, NCH, 6], FP32))
        small = enter(nc.sbuf_tensor("small", [P, 2, 8], FP32))
        eps = enter(nc.sbuf_tensor("eps_p", [P, 1], FP32))
        halves = enter(nc.sbuf_tensor("halves", [P, PER], FP32))
        to_table = enter(nc.sbuf_tensor("to_table", [P, PER, ROWLEN], FP32))
        w_emb_t = enter(nc.sbuf_tensor("w_emb_t", [C, PER, C], FP32))
        w_att = enter(nc.sbuf_tensor("w_att", [C, 2], FP32))
        half_ps = enter(nc.psum_tensor("half_ps", [P, 4, 512], FP32))
        table_ps = enter(nc.psum_tensor("table_ps", [P, TRING, 512], FP32))
        const_loaded = enter(nc.semaphore("p_const"))
        cleared = enter(nc.semaphore("p_cleared"))
        shares_made = enter(nc.semaphore("p_shares"))
        const_ready = enter(nc.semaphore("p_ready"))
        chain = enter(nc.semaphore("p_chain"))
        chain_act = enter(nc.semaphore("p_chain_act"))
        loaded0 = enter(nc.semaphore("p_loaded0"))
        loaded1 = enter(nc.semaphore("p_loaded1"))
        stored0 = enter(nc.semaphore("p_stored0"))
        stored1 = enter(nc.semaphore("p_stored1"))
        moments_ready = enter(nc.semaphore("p_moments"))
        std_ready = enter(nc.semaphore("p_std"))
        coef_ready = enter(nc.semaphore("p_coef"))
        feat_ready = enter(nc.semaphore("p_feat"))
        norm_ready = enter(nc.semaphore("p_norm"))
        rnorm_ready = enter(nc.semaphore("p_rnorm"))
        unit_ready = enter(nc.semaphore("p_unit"))
        squares_ready = enter(nc.semaphore("p_squares"))
        base_ready = enter(nc.semaphore("p_base"))
        half_made = enter(nc.semaphore("p_half_made"))
        half_ready = enter(nc.semaphore("p_half"))
        table_made = enter(nc.semaphore("p_table_made"))
        table_ready = enter(nc.semaphore("p_table"))
        block = enter(nc.Block())
        loaded, stored = [loaded0, loaded1], [stored0, stored1]
        mean, var, std, scale, shift, sumsq, norm, rnorm = range(8)

        def col(par, i):
            return small[:, par, i:i + 1]

        @block.sync
        def _(sp):
            for par in range(2):
                sp.sem_inc(stored[par], 16 * STORES)
            for b in range(PER):
                sp.dma_start(bias_sb[C * b:C * (b + 1), :], bias[:, :]).then_inc(const_loaded, 16)
                with nc.allow_non_contiguous_dma(reason="a small weight"):
                    sp.dma_start(w_emb_t[:, b, :], W_emb.rearrange("c k -> k c")).then_inc(const_loaded, 16)
            for h in range(2):
                sp.dma_start(w_att[:, 1 - h:2 - h], W_att[h * C:(h + 1) * C, :]).then_inc(const_loaded, 16)
            with sp.Fori(0, GROUPS // 2) as i:
                for par in range(2):
                    g = i * 2 + par
                    sp.wait_ge(feat_ready, g + 1)
                    for b in range(PER):
                        sp.dma_start(feat[:, bass.ds((g * PER + b) * N, N)], feat_sb[C * b:C * (b + 1), par, :]).then_inc(stored[par], 16)
                    sp.wait_ge(base_ready, g + 1)
                    sp.dma_start(base_rows[bass.ds(g * P, P), :], x_sb[:, par, :]).then_inc(stored[par], 16)
                    sp.wait_ge(unit_ready, g + 1)
                    for b in range(PER):
                        sp.dma_start(unit[:, bass.ds((g * PER + b) * N, N)], unit_sb[C * b:C * (b + 1), par, :]).then_inc(stored[par], 16)
                    sp.wait_ge(table_ready, g * TBANKS + (TBANKS + 1))
                    for b in range(PER):
                        sp.dma_start(table[bass.ds((g * PER + b) * N, N), :].rearrange("(p k) c -> p (k c)", k=TSTEP),
                                       table_sb[:, par, b, :, :].rearrange("p k c -> p (k c)")).then_inc(stored[par], 16)
                    sp.wait_ge(half_ready, g * 2 + 3)
                    sp.dma_start(half_sq[bass.ds(g * PER * N, PER * N)].rearrange("(b n) -> b n", n=N), half_sb[:, :]).then_inc(stored[par], 16)
            for par in range(2):
                sp.wait_ge(stored[par], 16 * STORES * (GROUPS // 2 + 1))

        @block.vector
        def _(dve):
            nc.vector.memset(eps[:], EPS).then_inc(chain, 1)
            nc.vector.memset(halves[:], 0.0).then_inc(chain, 1)
            nc.vector.memset(to_table[:], 0.0).then_inc(cleared, 1)
            dve.wait_ge(chain, 2)
            for b in range(PER):
                nc.vector.memset(halves[C * b:C * (b + 1), b:b + 1], 0.5).then_inc(chain, 1)
            dve.wait_ge(shares_made, 1)
            dve.wait_ge(cleared, 2)
            for b in range(PER):
                nc.vector.tensor_copy(to_table[C * b:C * (b + 1), b, C:C + 2],
                                      half_ps[C * b:C * (b + 1), 0, 0:2]).then_inc(chain, 1)
            dve.wait_ge(chain, 2 + 2 * PER)
            dve.sem_clear(chain)
            dve.sem_inc(const_ready, 1)
            dve.wait_ge(const_loaded, 16 * (2 * PER + 2))
            with dve.Fori(0, GROUPS // 2) as i:
                for par in range(2):
                    g = i * 2 + par
                    dve.wait_ge(loaded[par], i * 32 + 32)
                    x1_g = x1_sb[:, par, :]
                    nc.vector.tensor_tensor(x1_g, x1_g, x_sb[:, par, :], ALU.add).then_inc(chain, 1)
                    dve.wait_ge(chain, 1)
                    nc.vector.tensor_tensor(x1_g, x1_g, bias_sb[:, :], ALU.add).then_inc(chain, 1)
                    dve.wait_ge(chain, 2)
                    for c in range(NCH):
                        nc.vector.bn_stats(stats[:, c, :], x1_g[:, c * CH:(c + 1) * CH]).then_inc(chain, 1)
                    dve.wait_ge(chain, 2 + NCH)
                    nc.vector.bn_aggr(small[:, par, mean:var + 1], stats[:].rearrange("p a b -> p (a b)")).then_inc(moments_ready, 1)
                    dve.wait_ge(std_ready, g + 1)
                    nc.vector.reciprocal(col(par, scale), col(par, std)).then_inc(chain, 1)
                    dve.wait_ge(chain, 3 + NCH)
                    nc.vector.scalar_tensor_tensor(col(par, shift), col(par, mean), -1.0, col(par, scale),
                                                   ALU.mult, ALU.mult).then_inc(coef_ready, 1)
                    dve.wait_ge(norm_ready, g + 1)
                    nc.vector.tensor_scalar_max(col(par, rnorm), col(par, norm), 1e-12).then_inc(chain, 1)
                    dve.wait_ge(chain, 4 + NCH)
                    nc.vector.reciprocal(col(par, rnorm), col(par, rnorm)).then_inc(rnorm_ready, 1)
                    for t in range(TBANKS):
                        n = min(TBANK, TSTEP - t * TBANK)
                        dve.wait_ge(table_made, g * TBANKS + (t + 1))
                        nc.vector.tensor_copy(
                            table_sb[:, par, :, t * TBANK:t * TBANK + n, :].rearrange("p b k c -> p k b c"),
                            table_ps[0:TCOLS, t % TRING, 0:n * TW].rearrange("p (k b c) -> p k b c", k=n, b=PER)
                        ).then_inc(table_ready, 1)
                    dve.sem_clear(chain)

        @block.scalar
        def _(act):
            act.wait_ge(const_ready, 1)
            with act.Fori(0, GROUPS // 2) as i:
                for par in range(2):
                    g = i * 2 + par
                    act.wait_ge(moments_ready, g + 1)
                    nc.scalar.activation(col(par, std), col(par, var), ACT.Sqrt, bias=eps[:, 0:1]).then_inc(std_ready, 1)
                    act.wait_ge(coef_ready, g + 1)
                    nc.scalar.activation(feat_sb[:, par, :], x1_sb[:, par, :], ACT.Identity, bias=col(par, shift),
                                         scale=col(par, scale)).then_inc(feat_ready, 1)
                    act.wait_ge(half_made, g * NCH + 1)
                    act.wait_ge(feat_ready, g + 1)
                    nc.scalar.activation(squares[:, :], feat_sb[:, par, :], ACT.Square,
                                         accum_out=col(par, sumsq)).then_inc(chain_act, 1)
                    act.wait_ge(chain_act, 1)
                    nc.scalar.activation(col(par, norm), col(par, sumsq), ACT.Sqrt).then_inc(norm_ready, 1)
                    act.wait_ge(rnorm_ready, g + 1)
                    nc.scalar.activation(unit_sb[:, par, :], feat_sb[:, par, :], ACT.Copy,
                                         scale=col(par, rnorm)).then_inc(unit_ready, 1)
                    nc.scalar.activation(squares[:, :], feat_sb[:, par, :], ACT.Square,
                                         scale=col(par, rnorm)).then_inc(squares_ready, 1)
                    if par:
                        act.wait_ge(stored[0], (i + 2) * (16 * STORES))
                    else:
                        act.wait_ge(stored[1], (i + 1) * (16 * STORES))
                    for c0, n in ((0, 4), (4, 3)):
                        act.wait_ge(half_made, g * NCH + (c0 + n + 1))
                        nc.scalar.activation(half_sb[:, c0 * CH:(c0 + n) * CH].rearrange("p (a b) -> p a b", b=CH),
                                             half_ps[0:PER, 0:n, 0:CH], ACT.Copy).then_inc(half_ready, 1)
                    act.sem_clear(chain_act)

        @block.tensor
        def _(pe):
            pe.wait_ge(const_loaded, 16 * (2 * PER + 2))
            nc.tensor.matmul(half_ps[:, 0, 0:2], w_emb_t[:].rearrange("k b c -> k (b c)"), w_att[:], start=True, stop=True).then_inc(shares_made, 1)
            pe.sem_inc(half_made, 1)
            pe.wait_ge(const_ready, 1)
            with pe.Fori(0, GROUPS // 2) as i:
                for par in range(2):
                    g = i * 2 + par
                    pe.wait_ge(feat_ready, g + 1)
                    for t in range(TBANKS):
                        if t >= TRING:
                            pe.wait_ge(table_ready, g * TBANKS + (t - TRING + 2))
                        else:
                            pe.wait_ge(table_ready, g * TBANKS + 1)
                        for k in range(t * TBANK, min((t + 1) * TBANK, TSTEP)):
                            at = (k - t * TBANK) * TW
                            last = nc.tensor.matmul(table_ps[0:TCOLS, t % TRING, at:at + TW],
                                                    feat_sb[:, par, k::TSTEP], to_table[:].rearrange("p b c -> p (b c)"),
                                                    start=True, stop=True)
                        last.then_inc(table_made, 1)
                    pe.wait_ge(squares_ready, g + 1)
                    for c in range(NCH):
                        pe.wait_ge(half_ready, g * 2 + (1 if c < 4 else 2))
                        nc.tensor.matmul(half_ps[0:PER, c % 4, 0:CH], halves[:], squares[:, c * CH:(c + 1) * CH],
                                         start=True, stop=True).then_inc(half_made, 1)

        @block.gpsimd
        def _(pool):
            pool.sem_inc(half_ready, 1)
            pool.sem_inc(table_ready, 1)
            pool.wait_ge(cleared, 1)
            nc.gpsimd.affine_select(out=to_table[:, :, 0:C], in_=to_table[:, :, 0:C], compare_op=ALU.not_equal, fill=1.0,
                                    base=0, pattern=[[-C, PER], [-1, C]], channel_multiplier=1).then_inc(cleared, 1)
            with pool.Fori(0, GROUPS // 2) as i:
                for par in range(2):
                    g = i * 2 + par
                    pool.wait_ge(stored[par], (i + 1) * (16 * STORES))
                    pool.dma_start(x1_sb[:, par, :], conv_rows[bass.ds(g * P, P), :]).then_inc(loaded[par], 16)
                    pool.dma_start(x_sb[:, par, :], x_rows[bass.ds(g * P, P), :]).then_inc(loaded[par], 16)
                    pool.wait_ge(feat_ready, g + 1)
                    nc.gpsimd.tensor_tensor(x_sb[:, par, :], x1_sb[:, par, :], feat_sb[:, par, :], ALU.add).then_inc(base_ready, 1)


TILES = PER * N // P
HALF_TILES = TILES // 2
TAIL = N % P
FULL = N // P
TURN_LAG = 3
ATT_LAG = 2
PEEL = 4


def each_tile(engine, body, between=None):
    for half in range(2):
        first = half * HALF_TILES
        b = 2 * half
        for k in range(first, first + PEEL):
            body(k, k % 2, k // 2, b)
        if between is not None:
            between(half)
        for k0, count, batch in ((first + PEEL, FULL - PEEL, b), (first + FULL, 1, None), (first + FULL + 1, FULL, b + 1)):
            if batch is None:
                body(k0, k0 % 2, k0 // 2, (b, b + 1))
                continue
            with engine.Fori(0, count // 2) as i:
                for u in range(2):
                    k = k0 + u
                    body(i * 2 + k, k % 2, i + k // 2, batch)


def attend(nc, feat, unit, half_sq, table, W_emb, b_emb, W_att, b_att, W_conv, b_conv, y):
    BANK = 512
    BANKS = [(c, min(BANK, N - c)) for c in range(0, N, BANK)]
    NB = len(BANKS)
    LAST = NB * BANK
    KD = C + 2
    F0 = 64
    LOADS = 4
    COLS = PER * N
    H8 = NEIGHBOURS // 2
    PART = 224
    PARTS = N // PART
    PASSED = NEIGHBOURS
    FLAG = LAST + BANK - 1
    NEVER = -3.0e38
    with ExitStack() as stack:
        enter = stack.enter_context
        queries = enter(nc.sbuf_tensor("queries", [KD, 2, P], FP32))
        points = enter(nc.sbuf_tensor("points", [KD, COLS], FP32))
        hidden = enter(nc.sbuf_tensor("hidden", [F0 + C, COLS], FP32))
        scores = enter(nc.sbuf_tensor("scores", [P, 2, N], FP32))
        found = enter(nc.sbuf_tensor("found", [P, PARTS, H8], FP32))
        rest = enter(nc.sbuf_tensor("rest", [P, PARTS * H8], FP32))
        best = enter(nc.sbuf_tensor("best", [P, NEIGHBOURS + 1], FP32))
        doubt = enter(nc.sbuf_tensor("doubt", [P, 2], FP32))
        ones = enter(nc.sbuf_tensor("ones", [P, 1], FP32))
        doubts = enter(nc.sbuf_tensor("doubts", [1, 1], U32))
        place = enter(nc.sbuf_tensor("place", [P, NEIGHBOURS], U32))
        found_row = enter(nc.sbuf_tensor("found_row", [P, NEIGHBOURS], FP32))
        swap = enter(nc.sbuf_tensor("swap", [P, NEIGHBOURS], FP32))
        own_row = enter(nc.sbuf_tensor("own_row", [P, TILES], FP32))
        own_number = enter(nc.sbuf_tensor("own_number", [P, TILES], U32))
        row = enter(nc.sbuf_tensor("row", [P, 2, NEIGHBOURS], U32))
        first_row = enter(nc.sbuf_tensor("first_row", [P, 6], FP32))
        near = enter(nc.sbuf_tensor("near", [P, 2, NEIGHBOURS, ROWLEN], FP32))
        own = enter(nc.sbuf_tensor("own", [P, TILES, ROWLEN], FP32))
        logit = enter(nc.sbuf_tensor("logit", [P, 2, 2, NEIGHBOURS], FP32))
        top = enter(nc.sbuf_tensor("top", [P, 1], FP32))
        expd = enter(nc.sbuf_tensor("expd", [P, 2, NEIGHBOURS], FP32))
        total = enter(nc.sbuf_tensor("total", [P, 2], FP32))
        inverse = enter(nc.sbuf_tensor("inverse", [P, 1], FP32))
        attn = enter(nc.sbuf_tensor("attn", [P, NEIGHBOURS], FP32))
        weighted = enter(nc.sbuf_tensor("weighted", [P, NEIGHBOURS, C], FP32))
        summed = enter(nc.sbuf_tensor("summed", [P, 2, C], FP32))
        y_sb = enter(nc.sbuf_tensor("y_sb", [C, 2, N], FP32))
        ident = enter(nc.sbuf_tensor("ident_a", [P, P], FP32))
        emb_bias = enter(nc.sbuf_tensor("emb_bias", [C + 1, 1], FP32))
        spread = enter(nc.sbuf_tensor("spread", [C + 1, P], FP32))
        att_own = enter(nc.sbuf_tensor("att_own", [C + 1, 1], FP32))
        att_other = enter(nc.sbuf_tensor("att_other", [C + 1, 1], FP32))
        att_bias = enter(nc.sbuf_tensor("att_bias", [P, 1], FP32))
        to_y = enter(nc.sbuf_tensor("to_y", [F0 + C, C], FP32))
        ps = enter(nc.psum_tensor("psum", [P, 8 * BANK], FP32))
        cleared = enter(nc.semaphore("a_cleared"))
        const_loaded = enter(nc.semaphore("a_const"))
        spread_ready = enter(nc.semaphore("a_spread"))
        bias_made = enter(nc.semaphore("a_bias"))
        const_ready = enter(nc.semaphore("a_ready"))
        ident_ready = enter(nc.semaphore("a_ident"))
        half0_loaded = enter(nc.semaphore("a_half0"))
        half1_loaded = enter(nc.semaphore("a_half1"))
        scored = enter(nc.semaphore("a_scored"))
        scores_in = enter(nc.semaphore("a_scores_in"))
        staged0 = enter(nc.semaphore("a_staged0"))
        staged1 = enter(nc.semaphore("a_staged1"))
        scores_free = enter(nc.semaphore("a_scores_free"))
        doubt_ready = enter(nc.semaphore("a_doubt"))
        doubts_made = enter(nc.semaphore("a_doubts_made"))
        doubts_in = enter(nc.semaphore("a_doubts_in"))
        own_in = enter(nc.semaphore("a_own_in"))
        numbered = enter(nc.semaphore("a_numbered"))
        rows_ready = enter(nc.semaphore("a_rows_ready"))
        near_free = enter(nc.semaphore("a_near_free"))
        pool_passed = enter(nc.semaphore("a_pool_passed"))
        pe_passed = enter(nc.semaphore("a_pe_passed"))
        dve_passed = enter(nc.semaphore("a_dve_passed"))
        near0a = enter(nc.semaphore("a_near0a"))
        near0b = enter(nc.semaphore("a_near0b"))
        near1a = enter(nc.semaphore("a_near1a"))
        near1b = enter(nc.semaphore("a_near1b"))
        logits_ready = enter(nc.semaphore("a_logits"))
        exp_ready = enter(nc.semaphore("a_exp"))
        summed_ready = enter(nc.semaphore("a_summed"))
        sums_turned = enter(nc.semaphore("a_turned"))
        sums_in = enter(nc.semaphore("a_sums_in"))
        y_made = enter(nc.semaphore("a_y_made"))
        y_in = enter(nc.semaphore("a_y_in"))
        y_stored0 = enter(nc.semaphore("a_y_stored0"))
        y_stored1 = enter(nc.semaphore("a_y_stored1"))
        chain = enter(nc.semaphore("a_chain"))
        block = enter(nc.Block())
        half_loaded, near_in, y_stored = [half0_loaded, half1_loaded], [(near0a, near0b), (near1a, near1b)], [y_stored0, y_stored1]
        staged = [staged0, staged1]
        STAGE_FREE, SCORES_FREE, BANKS_FREE, NEAR_FREE, SUMMED_FREE, SUMS_FREE, Y_FREE = 2 * NB, 2, NB, 2, 2, 3, 1
        YG = PER * NCH
        half_sq_row = half_sq.rearrange("(o n) -> o n", o=1)

        @block.sync
        def _(sp):
            sp.wait_ge(cleared, 9)
            with nc.allow_non_contiguous_dma(reason="a few small weights"):
                sp.dma_start(emb_bias[0:C, :], b_emb.rearrange("(k o) -> k o", o=1)).then_inc(const_loaded, 16)
                sp.dma_start(att_own[0:C, :], W_att[0:C, :]).then_inc(const_loaded, 16)
                sp.dma_start(att_own[C:C + 1, :], b_att.rearrange("(k o) -> k o", o=1)).then_inc(const_loaded, 16)
                sp.dma_start(att_other[0:C, :], W_att[C:2 * C, :]).then_inc(const_loaded, 16)
                sp.dma_start(to_y[0:C, :], W_conv[0:C, :]).then_inc(const_loaded, 16)
                sp.dma_start(to_y[C:C + 1, :], b_conv.rearrange("(o k) -> o k", o=1)).then_inc(const_loaded, 16)
                sp.dma_start(to_y[F0:F0 + C, :], W_conv[C:2 * C, :]).then_inc(const_loaded, 16)

            def load_half(g, half):
                sp.wait_ge(y_made, g * YG + (half + 1) * (YG // 2))
                cols = slice(half * 2 * N, (half + 1) * 2 * N)
                at = bass.ds(g * COLS + half * 2 * N, 2 * N)
                sp.dma_start(points[0:C, cols], unit[:, at]).then_inc(half_loaded[half], 16)
                sp.dma_start(hidden[0:C, cols], feat[:, at]).then_inc(half_loaded[half], 16)
                sp.dma_start(points[C:C + 1, cols], half_sq_row[:, at]).then_inc(half_loaded[half], 16)
                with nc.allow_non_contiguous_dma(reason="a table row for each partition"):
                    sp.dma_start(own[:, half * HALF_TILES:(half + 1) * HALF_TILES, :],
                                 table[at, :].rearrange("(k p) c -> p k c", p=P)).then_inc(half_loaded[half], 16)

            def group(g, last):
                def body(k, par, pair, batch):
                    tile = g * TILES + k
                    sp.wait_ge(scored, tile * NB + (STAGE_FREE - NB))
                    sp.dma_start(queries[0:C, par, :], unit[:, bass.ds(tile * P, P)]).then_inc(staged[par], 16)
                    sp.dma_start(queries[C + 1:C + 2, par, :], half_sq_row[:, bass.ds(tile * P, P)]).then_inc(staged[par], 16)

                def between(half):
                    if half == 0:
                        load_half(g, 1)
                    elif not last:
                        load_half(g + 1, 0)

                each_tile(sp, body, between)

            load_half(0, 0)
            with sp.Fori(0, GROUPS - 1) as g:
                group(g, False)
            group(GROUPS - 1, True)

        @block.gpsimd
        def _(pool):
            nc.gpsimd.iota(own_number[:], [[P, TILES]], base=0, channel_multiplier=1).then_inc(numbered, 1)
            pool.wait_ge(cleared, 9)
            nc.gpsimd.affine_select(out=ident[:], in_=ident[:], compare_op=ALU.not_equal, fill=1.0, base=0,
                                    pattern=[[-1, P]], channel_multiplier=1).then_inc(ident_ready, 1)
            with pool.Fori(0, GROUPS * TILES // 2) as i:
                for par in range(2):
                    tile = i * 2 + par
                    pool.wait_ge(near_free, tile + 1)
                    gate(pool, rows_ready, tile + 1, pool_passed)
                    for j in range(1, NEIGHBOURS):
                        pool.indirect_dma_start(near[:, par, j, :], None, table[:, :],
                                                bass.IndirectOffsetOnAxis(ap=row[:, par, j:j + 1], axis=0)).then_inc(near_in[par][j // H8], 16)

        @block.tensor
        def _(pe):
            pe.sem_inc(y_made, YG)
            pe.sem_inc(scored, STAGE_FREE)
            pe.wait_ge(const_loaded, 16 * 7)
            pe.wait_ge(spread_ready, 1)
            nc.tensor.matmul(ps[:, 0:1], spread[:], att_own[:], start=True, stop=False)
            nc.tensor.matmul(ps[:, 0:1], spread[:], att_other[:], start=False, stop=True).then_inc(bias_made, 1)
            pe.wait_ge(const_ready, 1)
            pe.wait_ge(ident_ready, 1)
            with pe.Fori(0, GROUPS) as g:

                def add_doubts(k, par):
                    tile = g * TILES + k
                    gate(pe, doubt_ready, tile + 1, pe_passed)
                    gate(pe, sums_in, tile + (SUMS_FREE - 2), pe_passed)
                    for i in range(2):
                        last = nc.tensor.matmul(ps[0:1, FLAG:FLAG + 1], ones[:], doubt[:, i:i + 1], start=i == 0, stop=i == 1)
                    last.then_inc(doubts_made, 1)
                    gate(pe, doubts_in, tile + 1, pe_passed)

                def turn(k, par):
                    tile = g * TILES + k
                    pe.wait_ge(summed_ready, tile + 1)
                    pe.wait_ge(sums_in, tile + SUMS_FREE)
                    nc.tensor.transpose(ps[0:C, LAST:LAST + P], summed[:, par, :], ident[:]).then_inc(sums_turned, 1)

                def convolve_1x1(half):
                    turned = TILES if half else HALF_TILES + PEEL - TURN_LAG
                    pe.wait_ge(sums_in, g * TILES + (turned + SUMS_FREE))
                    for c in range(2 * NCH):
                        at = half * 2 * N + c * CH
                        pe.wait_ge(y_in, g * YG + (half * (YG // 2) + c + Y_FREE))
                        nc.tensor.matmul(ps[0:C, LAST:LAST + CH], to_y[:], hidden[:, at:at + CH],
                                         start=True, stop=True).then_inc(y_made, 1)
                    gate(pe, y_in, g * YG + ((half + 1) * (YG // 2) + Y_FREE), pe_passed)

                def body(k, par, pair, batch):
                    tile = g * TILES + k
                    if isinstance(k, int) and k in (0, HALF_TILES):
                        pe.wait_ge(half_loaded[k // HALF_TILES], g * (16 * LOADS) + 16 * LOADS)
                    pe.wait_ge(staged[par], (g * (TILES // 2) + pair) * 32 + 32)
                    parts = [(0, P, batch)] if isinstance(batch, int) else [(0, TAIL, batch[0]), (TAIL, P - TAIL, batch[1])]
                    for c, (at, width) in enumerate(BANKS):
                        gate(pe, scores_in, tile * NB + (c + 1), pe_passed)
                        for r0, rows, b in parts:
                            last = nc.tensor.matmul(ps[r0:r0 + rows, at:at + width], queries[:, par, r0:r0 + rows],
                                                    points[:, b * N + at:b * N + at + width], start=True, stop=True)
                        last.then_inc(scored, 1)
                    if not isinstance(k, int) or k >= 1:
                        add_doubts(k - 1, 1 - par)
                    if not isinstance(k, int) or k >= TURN_LAG:
                        turn(k - TURN_LAG, (par + TURN_LAG) % 2)

                each_tile(pe, body, lambda half: convolve_1x1(0) if half else None)
                add_doubts(TILES - 1, (TILES - 1) % 2)
                for k in range(TILES - TURN_LAG, TILES):
                    turn(k, k % 2)
                convolve_1x1(1)

        @block.scalar
        def _(act):
            act.sem_inc(scores_in, BANKS_FREE)
            act.sem_inc(sums_in, SUMS_FREE)
            act.sem_inc(y_in, Y_FREE)
            for par in range(2):
                act.sem_inc(y_stored[par], 16)
            act.wait_ge(bias_made, 1)
            nc.scalar.activation(att_bias[:], ps[:, 0:1], ACT.Copy).then_inc(const_ready, 1)
            with act.Fori(0, GROUPS) as g:

                def copy_doubts(k):
                    act.wait_ge(doubts_made, g * TILES + k + 1)
                    nc.scalar.activation(doubts[:], ps[0:1, FLAG:FLAG + 1], ACT.Copy).then_inc(doubts_in, 1)

                def copy_own(k, par):
                    act.wait_ge(near_free, g * TILES + k + 1)
                    nc.scalar.activation(near[:, par, 0:1, :], own[:, bass.ds(k, 1), :], ACT.Copy).then_inc(own_in, 1)

                def exponentiate(k, par):
                    act.wait_ge(logits_ready, g * TILES + k + 1)
                    nc.scalar.activation(expd[:, par, :], logit[:, par, 1, :], ACT.Exp,
                                         accum_out=total[:, par:par + 1]).then_inc(exp_ready, 1)

                def finish(k, par):
                    tile = g * TILES + k
                    act.wait_ge(sums_turned, tile + (1 + SUMMED_FREE))
                    nc.scalar.activation(hidden[F0:F0 + C, bass.ds(k * P, P)], ps[0:C, LAST:LAST + P],
                                         ACT.Copy).then_inc(sums_in, 1)

                def store_y(half):
                    for b in range(2):
                        act.wait_ge(y_stored[b], g * 32 + (half + 1) * 16)
                        for c in range(NCH):
                            made = half * (YG // 2) + b * NCH + c + 1
                            act.wait_ge(y_made, g * YG + (made + YG))
                            nc.scalar.activation(y_sb[:, b, c * CH:(c + 1) * CH], ps[0:C, LAST:LAST + CH], ACT.Copy).then_inc(y_in, 1)
                        act.wait_ge(y_in, g * YG + (made + Y_FREE))
                        act.dma_start(y[bass.ds(g * PER + (2 * half + b), 1), :, :].rearrange("o c n -> (o c) n"),
                                      y_sb[:, b, :]).then_inc(y_stored[b], 16)

                def body(k, par, pair, batch):
                    tile = g * TILES + k
                    act.wait_ge(scores_free, tile + (SCORES_FREE - 1))
                    for c, (at, width) in enumerate(BANKS):
                        act.wait_ge(scored, tile * NB + (c + 1 + STAGE_FREE))
                        nc.scalar.activation(scores[:, par, at:at + width], ps[:, at:at + width], ACT.Copy).then_inc(scores_in, 1)
                    if not isinstance(k, int) or k >= TURN_LAG:
                        exponentiate(k - TURN_LAG, (par + TURN_LAG) % 2)
                    if not isinstance(k, int) or k >= 1:
                        copy_doubts(k - 1)
                    if not isinstance(k, int) or k >= TURN_LAG:
                        finish(k - TURN_LAG, (par + TURN_LAG) % 2)
                    if not isinstance(k, int) or k >= 1:
                        copy_own(k - 1, 1 - par)

                each_tile(act, body, lambda half: store_y(0) if half else None)
                for k in range(TILES - TURN_LAG, TILES):
                    exponentiate(k, k % 2)
                    if k == TILES - TURN_LAG:
                        copy_doubts(TILES - 1)
                    finish(k, k % 2)
                    if k == TILES - TURN_LAG:
                        copy_own(TILES - 1, (TILES - 1) % 2)
                store_y(1)
            for b in range(2):
                act.wait_ge(y_stored[b], 16 + 32 * GROUPS)

        @block.vector
        def _(dve):
            dve.sem_inc(scores_free, SCORES_FREE)
            dve.sem_inc(near_free, NEAR_FREE)
            dve.sem_inc(sums_turned, SUMMED_FREE)
            for t, value in ((ident, 0.0), (emb_bias, 1.0), (att_own, 0.0), (att_other, 0.0), (to_y, 0.0)):
                nc.vector.memset(t[:], value).then_inc(cleared, 1)
            nc.vector.memset(spread[:], 1.0).then_inc(chain, 1)
            nc.vector.memset(ones[:], 1.0).then_inc(cleared, 1)
            nc.vector.memset(queries[C:C + 2, :, :], -1.0).then_inc(cleared, 1)
            nc.vector.memset(points[C:C + 2, :], -1.0).then_inc(cleared, 1)
            nc.vector.memset(hidden[C:F0, :], 1.0).then_inc(cleared, 1)
            dve.wait_ge(const_loaded, 16 * 7)
            dve.wait_ge(chain, 1)
            nc.vector.tensor_scalar(spread[:], spread[:], emb_bias[:, 0:1], None, ALU.mult).then_inc(spread_ready, 1)
            dve.sem_clear(chain)
            columns = [(0, 0), (0, 1), (1, 1), (2, 2), (2, 3), (3, 3)]
            for i, (low, high) in enumerate(columns):
                nc.vector.memset(first_row[0:TAIL, i:i + 1], float(low * N)).then_inc(chain, 1)
                nc.vector.memset(first_row[TAIL:P, i:i + 1], float(high * N)).then_inc(chain, 1)
            dve.wait_ge(numbered, 1)
            nc.vector.tensor_copy(own_row[:], own_number[:]).then_inc(chain, 1)
            dve.wait_ge(chain, 2 * len(columns) + 1)
            dve.sem_clear(chain)
            dve.wait_ge(const_ready, 1)
            with dve.Fori(0, GROUPS) as g:
                steps = [0]

                def step(instruction):
                    instruction.then_inc(chain, 1)
                    steps[0] += 1
                    return steps[0]

                def logits(k, par, pair):
                    tile = g * TILES + k
                    for part, count in zip(near_in[par], (H8 - 1, H8)):
                        dve.wait_ge(part, (g * (TILES // 2) + pair + 1) * (16 * count))
                    dve.wait_ge(own_in, tile + 1)
                    raw, shifted = logit[:, par, 0, :], logit[:, par, 1, :]
                    n = step(nc.vector.tensor_scalar(raw, near[:, par, :, C], own[:, bass.ds(k, 1), C + 1], att_bias[:, 0:1],
                                                      ALU.add, ALU.add))
                    dve.wait_ge(chain, n)
                    n = step(nc.vector.scalar_tensor_tensor(raw, raw, 0.1, raw, ALU.mult, ALU.max))
                    dve.wait_ge(chain, n)
                    n = step(nc.vector.reduce_max(top[:], raw, AX.X))
                    dve.wait_ge(chain, n)
                    nc.vector.tensor_scalar(shifted, raw, top[:, 0:1], None, ALU.subtract).then_inc(logits_ready, 1)

                def sums(k, par):
                    tile = g * TILES + k
                    dve.wait_ge(exp_ready, tile + 1)
                    n = step(nc.vector.reciprocal(inverse[:], total[:, par:par + 1]))
                    dve.wait_ge(chain, n)
                    n = step(nc.vector.tensor_scalar(attn[:], expd[:, par, :], inverse[:, 0:1], None, ALU.mult))
                    dve.wait_ge(chain, n)
                    n = step(nc.vector.tensor_tensor(weighted[:], near[:, par, :, 0:C],
                                                     attn[:].rearrange("p (k o) -> p k o", o=1).to_broadcast([P, NEIGHBOURS, C]), ALU.mult))
                    dve.wait_ge(chain, n)
                    dve.sem_inc(near_free, 1)
                    dve.wait_ge(sums_turned, tile + (SUMMED_FREE - 1))
                    nc.vector.tensor_reduce(summed[:, par, :], weighted[:].rearrange("p k c -> p c k"), AX.X, ALU.add).then_inc(summed_ready, 1)

                def clear_chain():
                    dve.wait_ge(chain, steps[0])
                    dve.sem_clear(chain)
                    steps[0] = 0

                def body(k, par, pair, batch):
                    tile = g * TILES + k
                    lagged = not isinstance(k, int) or k >= ATT_LAG
                    column = columns.index((batch, batch) if isinstance(batch, int) else batch)
                    s = scores[:, par, :]
                    gate(dve, scores_in, tile * NB + (NB + BANKS_FREE), dve_passed)
                    for c in range(PARTS):
                        n = step(nc.vector.max(found[:, c, :], s[:, c * PART:(c + 1) * PART]))
                    if lagged:
                        logits(k - ATT_LAG, par, pair - 1)
                    found_all = found[:].rearrange("p a b -> p (a b)")
                    dve.wait_ge(chain, n)
                    n = step(nc.vector.max(best[:, 0:H8], found_all))
                    dve.wait_ge(chain, n)
                    n = step(nc.vector.match_replace(rest[:], best[:, 0:H8], found_all, NEVER))
                    dve.wait_ge(chain, n)
                    step(nc.vector.reduce_max(best[:, PASSED:PASSED + 1], found[:, :, H8 - 1], AX.X))
                    n = step(nc.vector.max(best[:, H8:NEIGHBOURS], rest[:]))
                    dve.wait_ge(chain, n)
                    nc.vector.tensor_tensor(doubt[:], best[:, H8::H8], best[:, H8 - 1:NEIGHBOURS:H8], ALU.is_ge).then_inc(doubt_ready, 1)
                    step(nc.vector.max_index(place[:, 0:H8], best[:, 0:H8], s))
                    if lagged:
                        sums(k - ATT_LAG, par)
                    before = steps[0]
                    gate(dve, doubts_in, tile + 1, dve_passed)
                    in_doubt = dve.value_load(doubts[0:1, 0:1], min_val=0, max_val=2 * P)
                    dve.wait_ge(chain, before)
                    with dve.If(in_doubt > 0):
                        nc.vector.match_replace(s, best[:, 0:H8], s, NEVER).then_inc(chain, 1)
                        dve.wait_ge(chain, before + 1)
                        nc.vector.max(best[:, H8:NEIGHBOURS], s).then_inc(chain, 1)
                        dve.wait_ge(chain, before + 2)
                        nc.vector.max_index(place[:, H8:], best[:, H8:NEIGHBOURS], s).then_inc(chain, 1)
                    with dve.Else():
                        nc.vector.max_index(place[:, H8:], best[:, H8:NEIGHBOURS], s).then_inc(chain, 3)
                    steps[0] += 3
                    dve.wait_ge(chain, steps[0])
                    dve.sem_inc(scores_free, 1)
                    n = step(nc.vector.tensor_scalar(found_row[:], place[:], first_row[:, column:column + 1], None, ALU.add))
                    dve.wait_ge(chain, n)
                    n = step(nc.vector.tensor_scalar(swap[:], found_row[:], -1.0, found_row[:, 0:1], ALU.mult, ALU.add))
                    dve.wait_ge(chain, n)
                    n = step(nc.vector.scalar_tensor_tensor(swap[:], found_row[:], own_row[:, bass.ds(k, 1)], swap[:],
                                                            ALU.is_equal, ALU.mult))
                    dve.wait_ge(chain, n)
                    nc.vector.tensor_tensor(row[:, par, :], found_row[:], swap[:], ALU.add).then_inc(rows_ready, 1)
                    clear_chain()

                each_tile(dve, body)
                for k in range(TILES - ATT_LAG, TILES):
                    logits(k, k % 2, k // 2)
                    sums(k, k % 2)
                dve.wait_ge(chain, steps[0])
                dve.wait_ge(rows_ready, g * TILES + TILES)
                for rows in (first_row, own_row):
                    step(nc.vector.tensor_scalar(rows[:], rows[:], float(PER * N), None, ALU.add))
                clear_chain()


def normalise_output(nc, y, base, gamma, beta, out):
    y_rows = y.rearrange("b c n -> (b c) n")
    base_rows = base.rearrange("b c n -> (b c) n")
    out_rows = out.rearrange("b c h w -> (b c) (h w)")
    with ExitStack() as stack:
        enter = stack.enter_context
        y_all = enter(nc.sbuf_tensor("y_all", [P, GROUPS, N], FP32))
        base_sb = enter(nc.sbuf_tensor("base_sb", [P, 4, N], FP32))
        stats = enter(nc.sbuf_tensor("stats_o", [P, GROUPS * NCH, 6], FP32))
        moments = enter(nc.sbuf_tensor("moments_o", [P, 2], FP32))
        small = enter(nc.sbuf_tensor("small_o", [P, 8], FP32))
        affine = enter(nc.sbuf_tensor("affine", [P, 2], FP32))
        average = enter(nc.sbuf_tensor("average", [P, P], FP32))
        average_ps = enter(nc.psum_tensor("average_ps", [P, 2], FP32))
        cleared = enter(nc.semaphore("o_cleared"))
        const_loaded = enter(nc.semaphore("o_const"))
        average_ready = enter(nc.semaphore("o_average"))
        chain = enter(nc.semaphore("o_chain"))
        averaged = enter(nc.semaphore("o_averaged"))
        std_ready = enter(nc.semaphore("o_std"))
        coef_ready = enter(nc.semaphore("o_coef"))
        relu_ready = enter(nc.semaphore("o_relu"))
        added = enter(nc.semaphore("o_added"))
        y_loaded = [enter(nc.semaphore(f"o_y{g}")) for g in range(GROUPS)]
        base_loaded = [enter(nc.semaphore(f"o_b{g}")) for g in range(GROUPS)]
        stored = [enter(nc.semaphore(f"o_s{g}")) for g in range(GROUPS)]
        block = enter(nc.Block())
        mean, second, dev, std, scale, shift, eps, var = range(8)

        def col(i):
            return small[:, i:i + 1]

        @block.sync
        def _(sp):
            for b in range(PER):
                for i, src in enumerate((gamma, beta)):
                    sp.dma_start(affine[C * b:C * (b + 1), i:i + 1], src.rearrange("(c o) -> c o", o=1)).then_inc(const_loaded, 16)
            for g in range(GROUPS):
                sp.dma_start(y_all[:, g, :], y_rows[g * P:(g + 1) * P, :]).then_inc(y_loaded[g], 16)
            for g in range(GROUPS):
                if g >= 4:
                    sp.wait_ge(stored[g - 4], 16)
                sp.dma_start(base_sb[:, g % 4, :], base_rows[g * P:(g + 1) * P, :]).then_inc(base_loaded[g], 16)

        @block.gpsimd
        def _(pool):
            nc.gpsimd.memset(average[:], 0.0).then_inc(average_ready, 1)
            for n, d in enumerate(range(1 - PER, PER)):
                pool.wait_ge(average_ready, n + 1)
                nc.gpsimd.affine_select(out=average[:], in_=average[:], compare_op=ALU.not_equal, fill=1.0 / PER,
                                        base=C * d, pattern=[[-1, P]], channel_multiplier=1).then_inc(average_ready, 1)
            for g in range(GROUPS):
                pool.wait_ge(added, g + 1)
                pool.dma_start(out_rows[g * P:(g + 1) * P, :], y_all[:, g, :]).then_inc(stored[g], 16)
            for g in range(GROUPS):
                pool.wait_ge(stored[g], 16)

        @block.vector
        def _(dve):
            steps = [0]

            def link(instruction):
                steps[0] += 1
                instruction.then_inc(chain, 1)
                dve.wait_ge(chain, steps[0])

            link(nc.vector.memset(col(eps), EPS))
            for g in range(GROUPS):
                dve.wait_ge(y_loaded[g], 16)
                for c in range(NCH):
                    nc.vector.bn_stats(stats[:, g * NCH + c, :], y_all[:, g, c * CH:(c + 1) * CH]).then_inc(chain, 1)
                    steps[0] += 1
            dve.wait_ge(chain, steps[0])
            link(nc.vector.bn_aggr(moments[:], stats[:].rearrange("p a b -> p (a b)")))
            dve.sem_inc(cleared, 1)
            dve.wait_ge(averaged, 1)
            link(nc.vector.tensor_copy(col(mean), average_ps[:, 0:1]))
            link(nc.vector.tensor_tensor(col(dev), moments[:, 0:1], col(mean), ALU.subtract))
            link(nc.vector.tensor_tensor(col(second), col(dev), col(dev), ALU.mult))
            link(nc.vector.tensor_tensor(col(second), col(second), moments[:, 1:2], ALU.add))
            dve.sem_inc(cleared, 1)
            dve.wait_ge(averaged, 2)
            link(nc.vector.tensor_copy(col(var), average_ps[:, 1:2]))
            dve.sem_inc(cleared, 1)
            dve.wait_ge(std_ready, 1)
            link(nc.vector.reciprocal(col(scale), col(std)))
            dve.wait_ge(const_loaded, 16 * 2 * PER)
            link(nc.vector.tensor_tensor(col(scale), col(scale), affine[:, 0:1], ALU.mult))
            link(nc.vector.tensor_tensor(col(shift), col(scale), col(mean), ALU.mult))
            link(nc.vector.tensor_tensor(col(shift), affine[:, 1:2], col(shift), ALU.subtract))
            dve.sem_inc(coef_ready, 1)
            for g in range(GROUPS):
                dve.wait_ge(relu_ready, g + 1)
                dve.wait_ge(base_loaded[g], 16)
                nc.vector.tensor_tensor(y_all[:, g, :], y_all[:, g, :], base_sb[:, g % 4, :], ALU.add).then_inc(added, 1)

        @block.tensor
        def _(pe):
            pe.wait_ge(average_ready, 2 * PER)
            pe.wait_ge(cleared, 1)
            nc.tensor.matmul(average_ps[:, 0:1], average[:], moments[:, 0:1], start=True, stop=True).then_inc(averaged, 1)
            pe.wait_ge(cleared, 2)
            nc.tensor.matmul(average_ps[:, 1:2], average[:], col(second), start=True, stop=True).then_inc(averaged, 1)

        @block.scalar
        def _(act):
            act.wait_ge(cleared, 3)
            nc.scalar.activation(col(std), col(var), ACT.Sqrt, bias=col(eps)).then_inc(std_ready, 1)
            act.wait_ge(coef_ready, 1)
            for g in range(GROUPS):
                nc.scalar.activation(y_all[:, g, :], y_all[:, g, :], ACT.Relu, bias=col(shift), scale=col(scale)).then_inc(relu_ready, 1)


def build(nc, x, weight, bias, W_emb, b_emb, W_att, b_att, W_conv, b_conv, gamma, beta, out):
    xg = nc.dram_tensor("xg", [C, HP, BATCH, WP], FP32).ap()
    conv, base, y = (nc.dram_tensor(name, [BATCH, C, N], FP32).ap() for name in ("conv", "base", "y"))
    feat, unit = (nc.dram_tensor(name, [C, BATCH * N], FP32).ap() for name in ("feat", "unit"))
    half_sq = nc.dram_tensor("half_sq", [BATCH * N], FP32).ap()
    table = nc.dram_tensor("table", [BATCH * N, ROWLEN], FP32).ap()
    normalise_input(nc, x, xg)
    convolve(nc, weight, xg, conv)
    prepare(nc, x, conv, bias, W_emb, W_att, feat, unit, base, half_sq, table)
    attend(nc, feat, unit, half_sq, table, W_emb, b_emb, W_att, b_att, W_conv, b_conv, y)
    normalise_output(nc, y, base, gamma, beta, out)


_INS = ["x", "L0_conv_weight", "L0_conv_bias", "L1_conv_W_emb", "L1_conv_b_emb", "L1_conv_W_att", "L1_conv_b_att",
        "L1_conv_W_conv", "L1_conv_b_conv", "L1_conv_gamma", "L1_conv_beta"]
_OUTS = [((BATCH, C, H, W), "float32")]


def kernel(**inputs):
    import numpy as _np
    import concourse.bacc as _bacc
    from concourse import mybir as _mybir
    from concourse.bass_utils import run_bass_kernel_spmd as _run

    nc = _bacc.Bacc("TRN2", target_bir_lowering=False, num_devices=1)
    arrays, args = {}, []
    for name in _INS:
        a = _np.ascontiguousarray(inputs[name])
        arrays[f"in_{name}_dram"] = a
        args.append(nc.dram_tensor(f"in_{name}_dram", a.shape, _mybir.dt.from_np(a.dtype), kind="ExternalInput").ap())
    for i, (shape, dtype) in enumerate(_OUTS):
        dt = _mybir.dt.from_np(_np.dtype(dtype))
        args.append(nc.dram_tensor(f"out_{i}_dram", shape, dt, kind="ExternalOutput").ap())
    build(nc, *args)
    r = _run(nc, [arrays], core_ids=[0])
    return r.results[0]["out_0_dram"]
```

```python
from contextlib import ExitStack

import concourse.bass as bass
from concourse import mybir

FP32 = mybir.dt.float32
U32 = mybir.dt.uint32
ALU = mybir.AluOpType
ACT = mybir.ActivationFunctionType
AX = mybir.AxisListType

BATCH, C, H, W = 32, 32, 56, 56
N = H * W
K = 3
IN_DIM = C * K * K
NEIGHBOURS = 16
P = 128
PER = P // C
GROUPS = BATCH // PER
HP, WP = H + 2, W + 2
EPS = 1e-5
CH = 448
NCH = N // CH
QN = N // PER
QH = H // PER
ROWLEN = C + 2
TCOLS = 112
TSTEP = N // TCOLS


def gate(engine, sem, value, passed):
    engine.wait_ge(sem, value)
    engine.sem_inc(passed, 1)


def normalise_input(nc, x, xg):
    x_rows = x.rearrange("b c h w -> (b c) (h w)")
    with ExitStack() as stack:
        enter = stack.enter_context
        x_in = enter(nc.sbuf_tensor("x_in", [P, 2, N], FP32))
        padded = enter(nc.sbuf_tensor("padded", [P, 2, H, WP], FP32))
        stats = enter(nc.sbuf_tensor("stats", [P, 2, NCH, 6], FP32))
        moments = enter(nc.sbuf_tensor("moments", [P, 2, 2], FP32))
        std = enter(nc.sbuf_tensor("std", [P, 2], FP32))
        scale = enter(nc.sbuf_tensor("scale", [P, 2], FP32))
        shift = enter(nc.sbuf_tensor("shift", [P, 2], FP32))
        eps = enter(nc.sbuf_tensor("eps", [P, 1], FP32))
        zero_row = enter(nc.sbuf_tensor("zero_row", [C, BATCH * WP], FP32))
        x_loaded0 = enter(nc.semaphore("n0_x_loaded0"))
        x_loaded1 = enter(nc.semaphore("n0_x_loaded1"))
        cleared = enter(nc.semaphore("n0_cleared"))
        chain = enter(nc.semaphore("n0_chain"))
        moments_ready = enter(nc.semaphore("n0_moments_ready"))
        std_ready = enter(nc.semaphore("n0_std_ready"))
        coef_ready = enter(nc.semaphore("n0_coef_ready"))
        normed = enter(nc.semaphore("n0_normed"))
        border_stored = enter(nc.semaphore("n0_border"))
        stored0 = enter(nc.semaphore("n0_stored0"))
        stored1 = enter(nc.semaphore("n0_stored1"))
        block = enter(nc.Block())
        x_loaded = [x_loaded0, x_loaded1]
        stored = [stored0, stored1]
        x_free_credit = 2

        @block.gpsimd
        def _(pool):
            with pool.Fori(0, GROUPS // 2) as i:
                for par in range(2):
                    g = i * 2 + par
                    pool.wait_ge(normed, g + 1)
                    pool.dma_start(x_in[:, par, :], x_rows[bass.ds(g * P, P), :]).then_inc(x_loaded[par], 16)

        @block.vector
        def _(dve):
            nc.vector.memset(padded[:], 0.0).then_inc(cleared, 1)
            nc.vector.memset(eps[:], EPS).then_inc(cleared, 1)
            nc.vector.memset(zero_row[:], 0.0).then_inc(cleared, 1)
            with dve.Fori(0, GROUPS // 2) as i:
                for par in range(2):
                    g = i * 2 + par
                    dve.wait_ge(x_loaded[par], 16 * i + 16)
                    for c in range(NCH):
                        nc.vector.bn_stats(stats[:, par, c, :], x_in[:, par, c * CH:(c + 1) * CH]).then_inc(chain, 1)
                    dve.wait_ge(chain, NCH)
                    nc.vector.bn_aggr(moments[:, par, :], stats[:, par, :, :].rearrange("p a b -> p (a b)")).then_inc(moments_ready, 1)
                    dve.wait_ge(std_ready, g + 1)
                    nc.vector.reciprocal(scale[:, par:par + 1], std[:, par:par + 1]).then_inc(chain, 1)
                    dve.wait_ge(chain, NCH + 1)
                    nc.vector.scalar_tensor_tensor(shift[:, par:par + 1], moments[:, par, 0:1], -1.0, scale[:, par:par + 1],
                                                   ALU.mult, ALU.mult).then_inc(coef_ready, 1)
                    dve.sem_clear(chain)

        @block.scalar
        def _(act):
            act.sem_inc(normed, x_free_credit)
            act.wait_ge(cleared, 3)
            with act.Fori(0, GROUPS // 2) as i:
                for par in range(2):
                    g = i * 2 + par
                    act.wait_ge(moments_ready, g + 1)
                    nc.scalar.activation(std[:, par:par + 1], moments[:, par, 1:2], ACT.Sqrt, bias=eps[:, 0:1]).then_inc(std_ready, 1)
                    act.wait_ge(coef_ready, g + 1)
                    act.wait_ge(stored[par], 16 * PER * (i + 1))
                    nc.scalar.activation(padded[:, par, :, 1:1 + W], x_in[:, par, :].rearrange("p (h w) -> p h w", w=W),
                                         ACT.Identity, bias=shift[:, par:par + 1], scale=scale[:, par:par + 1]).then_inc(normed, 1)

        @block.sync
        def _(sp):
            for par in range(2):
                sp.sem_inc(stored[par], 16 * PER)
            sp.wait_ge(cleared, 3)
            sp.dma_start(xg[:, 0, :, :].rearrange("c b w -> c (b w)"), zero_row[:, :]).then_inc(border_stored, 16)
            sp.dma_start(xg[:, HP - 1, :, :].rearrange("c b w -> c (b w)"), zero_row[:, :]).then_inc(border_stored, 16)
            with sp.Fori(0, GROUPS // 2) as i:
                for par in range(2):
                    g = i * 2 + par
                    sp.wait_ge(normed, g + 1 + x_free_credit)
                    for j in range(PER):
                        sp.dma_start(xg[:, 1:1 + H, bass.ds(g * PER + j, 1), :].rearrange("c h b w -> c h (b w)"),
                                       padded[C * j:C * (j + 1), par, :, :]).then_inc(stored[par], 16)
            sp.wait_ge(border_stored, 32)
            for par in range(2):
                sp.wait_ge(stored[par], 16 * PER * (GROUPS // 2 + 1))


def convolve(nc, weight, xg, conv):
    SLOTS = 4
    AHEAD = 2
    CHUNKS = W // (2 * SLOTS)
    KC = K * C
    with ExitStack() as stack:
        enter = stack.enter_context
        windows = enter(nc.sbuf_tensor("windows", [KC, 2, PER, BATCH * WP], FP32))
        w_in = enter(nc.sbuf_tensor("w_in", [P, 2, SLOTS, IN_DIM], FP32))
        w_turned = enter(nc.sbuf_tensor("w_turned", [KC, 4, K * P], FP32))
        conv_sb = enter(nc.sbuf_tensor("conv_sb", [P, BATCH, QN], FP32))
        ident = enter(nc.sbuf_tensor("ident_c", [P, P], FP32))
        w_ps = enter(nc.psum_tensor("w_ps", [P, SLOTS, 512], FP32))
        conv_ps = enter(nc.psum_tensor("conv_ps", [P, 2, SLOTS, P], FP32))
        ident_ready = enter(nc.semaphore("c_ident"))
        win0 = enter(nc.semaphore("c_win0"))
        win1 = enter(nc.semaphore("c_win1"))
        w0 = enter(nc.semaphore("c_w0"))
        w1 = enter(nc.semaphore("c_w1"))
        turned = enter(nc.semaphore("c_turned"))
        wt_ready = enter(nc.semaphore("c_wt_ready"))
        multiplied = enter(nc.semaphore("c_multiplied"))
        copied = enter(nc.semaphore("c_copied"))
        out_stored = enter(nc.semaphore("c_out"))
        passed = enter(nc.semaphore("c_passed"))
        block = enter(nc.Block())
        win_loaded, w_loaded = [win0, win1], [w0, w1]
        xg_rows = xg.rearrange("c h b w -> c h (b w)")
        weight_rows = weight.rearrange("o p i -> o (p i)")
        TURN_FREE, WT_FREE, MUL_FREE, COPY_FREE = 2 * SLOTS, SLOTS, 2 * W, 2

        def each_half(engine, body):
            with engine.Fori(0, QH // 2) as t:
                for r in range(2):
                    row = t * 2 + r
                    body(row, None, None, r, None)
                    with engine.Fori(0, CHUNKS) as j:
                        for u in range(2):
                            body(row, (row * CHUNKS + j) * (2 * SLOTS) + u * SLOTS, j, r, u)

        @block.sync
        def _(sp):
            def body(row, before, j, r, u):
                if u is None:
                    sp.wait_ge(multiplied, row * W + W)
                    for k in range(K):
                        sp.dma_start(windows[k:KC:K, r, :, :],
                                     xg_rows[:, bass.ds(row + k, PER, QH), :]).then_inc(win_loaded[r], 16)
                    return
                sp.wait_ge(turned, before + SLOTS)
                for q in range(PER):
                    at = (row * W + j * (2 * SLOTS) + (u * SLOTS + q * QN)) * IN_DIM
                    sp.dma_start(w_in[C * q:C * (q + 1), u, :, :].rearrange("o s i -> o (s i)"),
                                 weight_rows[:, bass.ds(at, SLOTS * IN_DIM)]).then_inc(w_loaded[u], 16)

            each_half(sp, body)
            for q in range(PER):
                sp.wait_ge(copied, QN // SLOTS + COPY_FREE)
                sp.dma_start(conv[:, :, q * QN:(q + 1) * QN].rearrange("b c n -> c b n"),
                             conv_sb[C * q:C * (q + 1), :, :]).then_inc(out_stored, 16)
            sp.wait_ge(out_stored, 16 * PER)

        @block.gpsimd
        def _(pool):
            nc.gpsimd.memset(ident[:], 0.0).then_inc(ident_ready, 1)
            pool.wait_ge(ident_ready, 1)
            nc.gpsimd.affine_select(out=ident[:], in_=ident[:], compare_op=ALU.not_equal, fill=1.0, base=0,
                                    pattern=[[-1, P]], channel_multiplier=1).then_inc(ident_ready, 1)

        @block.tensor
        def _(pe):
            pe.sem_inc(turned, TURN_FREE)
            pe.sem_inc(multiplied, MUL_FREE)
            pe.wait_ge(ident_ready, 2)

            def turn(before, s, u):
                pe.wait_ge(wt_ready, before + (s + 1))
                for k in range(K):
                    last = nc.tensor.transpose(w_ps[0:KC, s, k * P:(k + 1) * P], w_in[:, u, s, k::K], ident[:])
                last.then_inc(turned, 1)

            def body(row, before, j, r, u):
                if u is None:
                    gate(pe, win_loaded[r], (row - r) * (8 * K) + 16 * K, passed)
                    return
                pe.wait_ge(w_loaded[u], (row * CHUNKS + j) * (16 * PER) + 16 * PER)
                for s in range(AHEAD):
                    turn(before, s, u)
                pe.wait_ge(copied, (row * CHUNKS + j) * 2 + (u + 1))
                for s in range(SLOTS):
                    if s + AHEAD < SLOTS:
                        turn(before, s + AHEAD, u)
                    pe.wait_ge(wt_ready, before + (s + 1 + WT_FREE))
                    for k in range(K):
                        x_k = windows[:, r, :, :].rearrange("p q (b w) -> p q b w", w=WP)[:, :, :, bass.ds(j * (2 * SLOTS) + (u * SLOTS + s + k), 1)]
                        last = nc.tensor.matmul(conv_ps[:, u, s, :], w_turned[:, s, k * P:(k + 1) * P], x_k,
                                                start=k == 0, stop=k == K - 1)
                    last.then_inc(multiplied, 1)

            each_half(pe, body)

        @block.scalar
        def _(act):
            act.sem_inc(wt_ready, WT_FREE)

            def body(row, before, j, r, u):
                if u is None:
                    return
                for s in range(SLOTS):
                    act.wait_ge(turned, before + (s + 1 + TURN_FREE))
                    act.wait_ge(multiplied, before + (s - SLOTS + 1 + MUL_FREE))
                    nc.scalar.activation(w_turned[:, s, :], w_ps[0:KC, s, 0:K * P], ACT.Copy).then_inc(wt_ready, 1)

            each_half(act, body)

        @block.vector
        def _(dve):
            dve.sem_inc(copied, COPY_FREE)

            def body(row, before, j, r, u):
                if u is None:
                    return
                dve.wait_ge(multiplied, before + (SLOTS + MUL_FREE))
                for q in range(PER):
                    rows = slice(C * q, C * (q + 1))
                    last = nc.vector.tensor_copy(
                        conv_sb[rows, :, bass.ds(row * W + (j * (2 * SLOTS) + u * SLOTS), SLOTS)],
                        conv_ps[rows, u, :, C * q:C * q + BATCH].rearrange("p s b -> p b s"))
                last.then_inc(copied, 1)

            each_half(dve, body)


def prepare(nc, x, conv, bias, W_emb, W_att, feat, unit, base, half_sq, table):
    conv_rows, base_rows = conv.rearrange("b c n -> (b c) n"), base.rearrange("b c n -> (b c) n")
    x_rows = x.rearrange("b c h w -> (b c) (h w)")
    TBANK = 3
    TBANKS = -(-TSTEP // TBANK)
    TRING = 4
    TW = PER * ROWLEN
    STORES = 2 + 3 * PER
    with ExitStack() as stack:
        enter = stack.enter_context
        x1_sb = enter(nc.sbuf_tensor("x1_sb", [P, 2, N], FP32))
        x_sb = enter(nc.sbuf_tensor("x_sb", [P, 2, N], FP32))
        feat_sb = enter(nc.sbuf_tensor("feat_sb", [P, 2, N], FP32))
        unit_sb = enter(nc.sbuf_tensor("unit_sb", [P, 2, N], FP32))
        squares = enter(nc.sbuf_tensor("squares", [P, N], FP32))
        bias_sb = enter(nc.sbuf_tensor("bias_sb", [P, N], FP32))
        table_sb = enter(nc.sbuf_tensor("table_sb", [TCOLS, 2, PER, TSTEP, ROWLEN], FP32))
        half_sb = enter(nc.sbuf_tensor("half_sb", [PER, N], FP32))
        stats = enter(nc.sbuf_tensor("stats_p", [P, NCH, 6], FP32))
        small = enter(nc.sbuf_tensor("small", [P, 2, 8], FP32))
        eps = enter(nc.sbuf_tensor("eps_p", [P, 1], FP32))
        halves = enter(nc.sbuf_tensor("halves", [P, PER], FP32))
        to_table = enter(nc.sbuf_tensor("to_table", [P, PER, ROWLEN], FP32))
        w_emb_t = enter(nc.sbuf_tensor("w_emb_t", [C, PER, C], FP32))
        w_att = enter(nc.sbuf_tensor("w_att", [C, 2], FP32))
        half_ps = enter(nc.psum_tensor("half_ps", [P, 4, 512], FP32))
        table_ps = enter(nc.psum_tensor("table_ps", [P, TRING, 512], FP32))
        const_loaded = enter(nc.semaphore("p_const"))
        cleared = enter(nc.semaphore("p_cleared"))
        shares_made = enter(nc.semaphore("p_shares"))
        const_ready = enter(nc.semaphore("p_ready"))
        chain = enter(nc.semaphore("p_chain"))
        chain_act = enter(nc.semaphore("p_chain_act"))
        loaded0 = enter(nc.semaphore("p_loaded0"))
        loaded1 = enter(nc.semaphore("p_loaded1"))
        stored0 = enter(nc.semaphore("p_stored0"))
        stored1 = enter(nc.semaphore("p_stored1"))
        moments_ready = enter(nc.semaphore("p_moments"))
        std_ready = enter(nc.semaphore("p_std"))
        coef_ready = enter(nc.semaphore("p_coef"))
        feat_ready = enter(nc.semaphore("p_feat"))
        norm_ready = enter(nc.semaphore("p_norm"))
        rnorm_ready = enter(nc.semaphore("p_rnorm"))
        unit_ready = enter(nc.semaphore("p_unit"))
        squares_ready = enter(nc.semaphore("p_squares"))
        base_ready = enter(nc.semaphore("p_base"))
        half_made = enter(nc.semaphore("p_half_made"))
        half_ready = enter(nc.semaphore("p_half"))
        table_made = enter(nc.semaphore("p_table_made"))
        table_ready = enter(nc.semaphore("p_table"))
        block = enter(nc.Block())
        loaded, stored = [loaded0, loaded1], [stored0, stored1]
        mean, var, std, scale, shift, sumsq, norm, rnorm = range(8)

        def col(par, i):
            return small[:, par, i:i + 1]

        @block.sync
        def _(sp):
            for par in range(2):
                sp.sem_inc(stored[par], 16 * STORES)
            for b in range(PER):
                sp.dma_start(bias_sb[C * b:C * (b + 1), :], bias[:, :]).then_inc(const_loaded, 16)
                with nc.allow_non_contiguous_dma(reason="a small weight"):
                    sp.dma_start(w_emb_t[:, b, :], W_emb.rearrange("c k -> k c")).then_inc(const_loaded, 16)
            for h in range(2):
                sp.dma_start(w_att[:, 1 - h:2 - h], W_att[h * C:(h + 1) * C, :]).then_inc(const_loaded, 16)
            with sp.Fori(0, GROUPS // 2) as i:
                for par in range(2):
                    g = i * 2 + par
                    sp.wait_ge(feat_ready, g + 1)
                    for b in range(PER):
                        sp.dma_start(feat[:, bass.ds((g * PER + b) * N, N)], feat_sb[C * b:C * (b + 1), par, :]).then_inc(stored[par], 16)
                    sp.wait_ge(base_ready, g + 1)
                    sp.dma_start(base_rows[bass.ds(g * P, P), :], x_sb[:, par, :]).then_inc(stored[par], 16)
                    sp.wait_ge(unit_ready, g + 1)
                    for b in range(PER):
                        sp.dma_start(unit[:, bass.ds((g * PER + b) * N, N)], unit_sb[C * b:C * (b + 1), par, :]).then_inc(stored[par], 16)
                    sp.wait_ge(table_ready, g * TBANKS + (TBANKS + 1))
                    for b in range(PER):
                        sp.dma_start(table[bass.ds((g * PER + b) * N, N), :].rearrange("(p k) c -> p (k c)", k=TSTEP),
                                       table_sb[:, par, b, :, :].rearrange("p k c -> p (k c)")).then_inc(stored[par], 16)
                    sp.wait_ge(half_ready, g * 2 + 3)
                    sp.dma_start(half_sq[bass.ds(g * PER * N, PER * N)].rearrange("(b n) -> b n", n=N), half_sb[:, :]).then_inc(stored[par], 16)
            for par in range(2):
                sp.wait_ge(stored[par], 16 * STORES * (GROUPS // 2 + 1))

        @block.vector
        def _(dve):
            nc.vector.memset(eps[:], EPS).then_inc(chain, 1)
            nc.vector.memset(halves[:], 0.0).then_inc(chain, 1)
            nc.vector.memset(to_table[:], 0.0).then_inc(cleared, 1)
            dve.wait_ge(chain, 2)
            for b in range(PER):
                nc.vector.memset(halves[C * b:C * (b + 1), b:b + 1], 0.5).then_inc(chain, 1)
            dve.wait_ge(shares_made, 1)
            dve.wait_ge(cleared, 2)
            for b in range(PER):
                nc.vector.tensor_copy(to_table[C * b:C * (b + 1), b, C:C + 2],
                                      half_ps[C * b:C * (b + 1), 0, 0:2]).then_inc(chain, 1)
            dve.wait_ge(chain, 2 + 2 * PER)
            dve.sem_clear(chain)
            dve.sem_inc(const_ready, 1)
            dve.wait_ge(const_loaded, 16 * (2 * PER + 2))
            with dve.Fori(0, GROUPS // 2) as i:
                for par in range(2):
                    g = i * 2 + par
                    dve.wait_ge(loaded[par], i * 32 + 32)
                    x1_g = x1_sb[:, par, :]
                    nc.vector.tensor_tensor(x1_g, x1_g, x_sb[:, par, :], ALU.add).then_inc(chain, 1)
                    dve.wait_ge(chain, 1)
                    nc.vector.tensor_tensor(x1_g, x1_g, bias_sb[:, :], ALU.add).then_inc(chain, 1)
                    dve.wait_ge(chain, 2)
                    for c in range(NCH):
                        nc.vector.bn_stats(stats[:, c, :], x1_g[:, c * CH:(c + 1) * CH]).then_inc(chain, 1)
                    dve.wait_ge(chain, 2 + NCH)
                    nc.vector.bn_aggr(small[:, par, mean:var + 1], stats[:].rearrange("p a b -> p (a b)")).then_inc(moments_ready, 1)
                    dve.wait_ge(std_ready, g + 1)
                    nc.vector.reciprocal(col(par, scale), col(par, std)).then_inc(chain, 1)
                    dve.wait_ge(chain, 3 + NCH)
                    nc.vector.scalar_tensor_tensor(col(par, shift), col(par, mean), -1.0, col(par, scale),
                                                   ALU.mult, ALU.mult).then_inc(coef_ready, 1)
                    dve.wait_ge(feat_ready, g + 1)
                    nc.vector.tensor_tensor(x_sb[:, par, :], x1_g, feat_sb[:, par, :], ALU.add).then_inc(base_ready, 1)
                    dve.wait_ge(norm_ready, g + 1)
                    nc.vector.tensor_scalar_max(col(par, rnorm), col(par, norm), 1e-12).then_inc(chain, 1)
                    dve.wait_ge(chain, 4 + NCH)
                    nc.vector.reciprocal(col(par, rnorm), col(par, rnorm)).then_inc(rnorm_ready, 1)
                    for t in range(TBANKS):
                        n = min(TBANK, TSTEP - t * TBANK)
                        dve.wait_ge(table_made, g * TBANKS + (t + 1))
                        nc.vector.tensor_copy(
                            table_sb[:, par, :, t * TBANK:t * TBANK + n, :].rearrange("p b k c -> p k b c"),
                            table_ps[0:TCOLS, t % TRING, 0:n * TW].rearrange("p (k b c) -> p k b c", k=n, b=PER)
                        ).then_inc(table_ready, 1)
                    dve.sem_clear(chain)

        @block.scalar
        def _(act):
            act.wait_ge(const_ready, 1)
            with act.Fori(0, GROUPS // 2) as i:
                for par in range(2):
                    g = i * 2 + par
                    act.wait_ge(moments_ready, g + 1)
                    nc.scalar.activation(col(par, std), col(par, var), ACT.Sqrt, bias=eps[:, 0:1]).then_inc(std_ready, 1)
                    act.wait_ge(coef_ready, g + 1)
                    nc.scalar.activation(feat_sb[:, par, :], x1_sb[:, par, :], ACT.Identity, bias=col(par, shift),
                                         scale=col(par, scale)).then_inc(feat_ready, 1)
                    act.wait_ge(half_made, g * NCH + 1)
                    act.wait_ge(feat_ready, g + 1)
                    nc.scalar.activation(squares[:, :], feat_sb[:, par, :], ACT.Square,
                                         accum_out=col(par, sumsq)).then_inc(chain_act, 1)
                    act.wait_ge(chain_act, 1)
                    nc.scalar.activation(col(par, norm), col(par, sumsq), ACT.Sqrt).then_inc(norm_ready, 1)
                    act.wait_ge(rnorm_ready, g + 1)
                    nc.scalar.activation(unit_sb[:, par, :], feat_sb[:, par, :], ACT.Copy,
                                         scale=col(par, rnorm)).then_inc(unit_ready, 1)
                    nc.scalar.activation(squares[:, :], feat_sb[:, par, :], ACT.Square,
                                         scale=col(par, rnorm)).then_inc(squares_ready, 1)
                    if par:
                        act.wait_ge(stored[0], (i + 2) * (16 * STORES))
                    else:
                        act.wait_ge(stored[1], (i + 1) * (16 * STORES))
                    for c0, n in ((0, 4), (4, 3)):
                        act.wait_ge(half_made, g * NCH + (c0 + n + 1))
                        nc.scalar.activation(half_sb[:, c0 * CH:(c0 + n) * CH].rearrange("p (a b) -> p a b", b=CH),
                                             half_ps[0:PER, 0:n, 0:CH], ACT.Copy).then_inc(half_ready, 1)
                    act.sem_clear(chain_act)

        @block.tensor
        def _(pe):
            pe.wait_ge(const_loaded, 16 * (2 * PER + 2))
            nc.tensor.matmul(half_ps[:, 0, 0:2], w_emb_t[:].rearrange("k b c -> k (b c)"), w_att[:], start=True, stop=True).then_inc(shares_made, 1)
            pe.sem_inc(half_made, 1)
            pe.wait_ge(const_ready, 1)
            with pe.Fori(0, GROUPS // 2) as i:
                for par in range(2):
                    g = i * 2 + par
                    pe.wait_ge(feat_ready, g + 1)
                    for t in range(TBANKS):
                        if t >= TRING:
                            pe.wait_ge(table_ready, g * TBANKS + (t - TRING + 2))
                        else:
                            pe.wait_ge(table_ready, g * TBANKS + 1)
                        for k in range(t * TBANK, min((t + 1) * TBANK, TSTEP)):
                            at = (k - t * TBANK) * TW
                            last = nc.tensor.matmul(table_ps[0:TCOLS, t % TRING, at:at + TW],
                                                    feat_sb[:, par, k::TSTEP], to_table[:].rearrange("p b c -> p (b c)"),
                                                    start=True, stop=True)
                        last.then_inc(table_made, 1)
                    pe.wait_ge(squares_ready, g + 1)
                    for c in range(NCH):
                        pe.wait_ge(half_ready, g * 2 + (1 if c < 4 else 2))
                        nc.tensor.matmul(half_ps[0:PER, c % 4, 0:CH], halves[:], squares[:, c * CH:(c + 1) * CH],
                                         start=True, stop=True).then_inc(half_made, 1)

        @block.gpsimd
        def _(pool):
            pool.sem_inc(half_ready, 1)
            pool.sem_inc(table_ready, 1)
            pool.wait_ge(cleared, 1)
            nc.gpsimd.affine_select(out=to_table[:, :, 0:C], in_=to_table[:, :, 0:C], compare_op=ALU.not_equal, fill=1.0,
                                    base=0, pattern=[[-C, PER], [-1, C]], channel_multiplier=1).then_inc(cleared, 1)
            with pool.Fori(0, GROUPS // 2) as i:
                for par in range(2):
                    g = i * 2 + par
                    pool.wait_ge(stored[par], (i + 1) * (16 * STORES))
                    pool.dma_start(x1_sb[:, par, :], conv_rows[bass.ds(g * P, P), :]).then_inc(loaded[par], 16)
                    pool.dma_start(x_sb[:, par, :], x_rows[bass.ds(g * P, P), :]).then_inc(loaded[par], 16)


TILES = PER * N // P
HALF_TILES = TILES // 2
TAIL = N % P
FULL = N // P
ROW_LAG = 1
ATT_LAG = 3
EXP_LAG = 4
TURN_LAG = 4
PEEL = 4


Y_STEPS = 2 * NCH
L_STEPS = 7


def each_tile(engine, body, between):

    def start(g, half):
        for k in range(half * HALF_TILES, half * HALF_TILES + PEEL):
            body(g, k, k % 2, k // 2, 2 * half, None, None)

    def run(g, k0, count, batch, y_half=None, steps=False, load_half=None):
        with engine.Fori(0, count // 2) as i:
            for u in range(2):
                k = k0 + u
                y_step = None if y_half is None else y_half + ((i * 2 + u) if steps else Y_STEPS,)
                load_step = None if load_half is None or u else load_half + (i,)
                body(g, i * 2 + k, k % 2, i + k // 2, batch, y_step, load_step)

    def others(g, half):
        first, b = half * HALF_TILES, 2 * half
        if half:
            y_half = (g, 0)
            load_half = None if isinstance(g, int) else (g + 1, 0)
        else:
            y_half = None if isinstance(g, int) else (g - 1, 1)
            load_half = (g, 1)
        run(g, first + PEEL, Y_STEPS, b, y_half, steps=True)
        between(g, half)
        run(g, first + PEEL + Y_STEPS, FULL - PEEL - Y_STEPS, b, y_half)
        body(g, first + FULL, (first + FULL) % 2, (first + FULL) // 2, (b, b + 1), None, None)
        run(g, first + FULL + 1, 2 * L_STEPS, b + 1, load_half=load_half)
        run(g, first + FULL + 1 + 2 * L_STEPS, FULL - 2 * L_STEPS, b + 1)

    start(0, 0)
    others(0, 0)
    with engine.Fori(0, GROUPS - 1) as g:
        start(g, 1)
        others(g, 1)
        start(g + 1, 0)
        others(g + 1, 0)
    start(GROUPS - 1, 1)
    others(GROUPS - 1, 1)


def begun(g, k, lag):
    return not (isinstance(g, int) and isinstance(k, int) and g * TILES + k < lag)


def earlier(k, lag):
    return k - lag + TILES if isinstance(k, int) and k < lag else k - lag


def attend(nc, feat, unit, half_sq, table, W_emb, b_emb, W_att, b_att, W_conv, b_conv, y):
    BANK = 512
    BANKS = [(c, min(BANK, N - c)) for c in range(0, N, BANK)]
    NB = len(BANKS)
    LAST = NB * BANK
    KD = C + 2
    F0 = 64
    LOADS = 4 * L_STEPS
    L_COLS = 2 * N // L_STEPS
    COLS = PER * N
    H8 = NEIGHBOURS // 2
    PART = 224
    PARTS = N // PART
    EARLY = 4
    PASSED = NEIGHBOURS
    FLAG = LAST + BANK - 1
    NEVER = -3.0e38
    ALL = GROUPS * TILES
    OWN_LAG = 2
    with ExitStack() as stack:
        enter = stack.enter_context
        queries = enter(nc.sbuf_tensor("queries", [KD, 2, P], FP32))
        points = enter(nc.sbuf_tensor("points", [KD, COLS], FP32))
        hidden = enter(nc.sbuf_tensor("hidden", [F0 + C, COLS], FP32))
        scores = enter(nc.sbuf_tensor("scores", [P, 2, N], FP32))
        found = enter(nc.sbuf_tensor("found", [P, PARTS, H8], FP32))
        rest = enter(nc.sbuf_tensor("rest", [P, PARTS * H8], FP32))
        best = enter(nc.sbuf_tensor("best", [P, NEIGHBOURS + 1], FP32))
        doubt = enter(nc.sbuf_tensor("doubt", [P, 2], FP32))
        ones = enter(nc.sbuf_tensor("ones", [P, 1], FP32))
        doubts = enter(nc.sbuf_tensor("doubts", [1, 1], U32))
        place = enter(nc.sbuf_tensor("place", [P, NEIGHBOURS], U32))
        placed = enter(nc.sbuf_tensor("placed", [P, NEIGHBOURS], FP32))
        swap = enter(nc.sbuf_tensor("swap", [P, NEIGHBOURS], FP32))
        own_place = enter(nc.sbuf_tensor("own_place", [P, TILES], FP32))
        own_number = enter(nc.sbuf_tensor("own_number", [P, TILES], U32))
        row = enter(nc.sbuf_tensor("row", [P, 2, NEIGHBOURS], U32))
        batch_row = enter(nc.sbuf_tensor("batch_row", [P, TILES], FP32))
        near = enter(nc.sbuf_tensor("near", [P, 2, NEIGHBOURS, ROWLEN], FP32))
        own = enter(nc.sbuf_tensor("own", [P, TILES, ROWLEN], FP32))
        logit = enter(nc.sbuf_tensor("logit", [P, 2, 2, NEIGHBOURS], FP32))
        top = enter(nc.sbuf_tensor("top", [P, 1], FP32))
        expd = enter(nc.sbuf_tensor("expd", [P, 2, NEIGHBOURS], FP32))
        total = enter(nc.sbuf_tensor("total", [P, 2], FP32))
        inverse = enter(nc.sbuf_tensor("inverse", [P, 1], FP32))
        attn = enter(nc.sbuf_tensor("attn", [P, NEIGHBOURS], FP32))
        weighted = enter(nc.sbuf_tensor("weighted", [P, NEIGHBOURS, C], FP32))
        summed = enter(nc.sbuf_tensor("summed", [P, 2, C], FP32))
        y_sb = enter(nc.sbuf_tensor("y_sb", [C, 2 * N], FP32))
        ident = enter(nc.sbuf_tensor("ident_a", [P, P], FP32))
        emb_bias = enter(nc.sbuf_tensor("emb_bias", [C + 1, 1], FP32))
        spread = enter(nc.sbuf_tensor("spread", [C + 1, P], FP32))
        att_own = enter(nc.sbuf_tensor("att_own", [C + 1, 1], FP32))
        att_other = enter(nc.sbuf_tensor("att_other", [C + 1, 1], FP32))
        att_bias = enter(nc.sbuf_tensor("att_bias", [P, 1], FP32))
        to_y = enter(nc.sbuf_tensor("to_y", [F0 + C, C], FP32))
        ps = enter(nc.psum_tensor("psum", [P, 8 * BANK], FP32))
        cleared = enter(nc.semaphore("a_cleared"))
        const_loaded = enter(nc.semaphore("a_const"))
        spread_ready = enter(nc.semaphore("a_spread"))
        bias_made = enter(nc.semaphore("a_bias"))
        const_ready = enter(nc.semaphore("a_ready"))
        ident_ready = enter(nc.semaphore("a_ident"))
        half0_loaded = enter(nc.semaphore("a_half0"))
        half1_loaded = enter(nc.semaphore("a_half1"))
        scored = enter(nc.semaphore("a_scored"))
        scores_in = enter(nc.semaphore("a_scores_in"))
        staged0 = enter(nc.semaphore("a_staged0"))
        staged1 = enter(nc.semaphore("a_staged1"))
        scores_free = enter(nc.semaphore("a_scores_free"))
        doubt_ready = enter(nc.semaphore("a_doubt"))
        doubts_made = enter(nc.semaphore("a_doubts_made"))
        doubts_in = enter(nc.semaphore("a_doubts_in"))
        own_in = enter(nc.semaphore("a_own_in"))
        numbered = enter(nc.semaphore("a_numbered"))
        rows_ready = enter(nc.semaphore("a_rows_ready"))
        near_free = enter(nc.semaphore("a_near_free"))
        pool_passed = enter(nc.semaphore("a_pool_passed"))
        pe_passed = enter(nc.semaphore("a_pe_passed"))
        dve_passed = enter(nc.semaphore("a_dve_passed"))
        near0a = enter(nc.semaphore("a_near0a"))
        near0b = enter(nc.semaphore("a_near0b"))
        near1a = enter(nc.semaphore("a_near1a"))
        near1b = enter(nc.semaphore("a_near1b"))
        logits_ready = enter(nc.semaphore("a_logits"))
        exp_ready = enter(nc.semaphore("a_exp"))
        summed_ready = enter(nc.semaphore("a_summed"))
        sums_turned = enter(nc.semaphore("a_turned"))
        sums_in = enter(nc.semaphore("a_sums_in"))
        y_made = enter(nc.semaphore("a_y_made"))
        y_in = enter(nc.semaphore("a_y_in"))
        y_stored0 = enter(nc.semaphore("a_y_stored0"))
        y_stored1 = enter(nc.semaphore("a_y_stored1"))
        chain = enter(nc.semaphore("a_chain"))
        block = enter(nc.Block())
        half_loaded, near_in, y_stored = [half0_loaded, half1_loaded], [(near0a, near0b), (near1a, near1b)], [y_stored0, y_stored1]
        staged = [staged0, staged1]
        STAGE_FREE, SCORES_FREE, BANKS_FREE, NEAR_FREE, SUMMED_FREE, SUMS_FREE, Y_FREE = 2 * NB, 2, NB, 2, 2, 4, 1
        YG = PER * NCH
        half_sq_row = half_sq.rearrange("(o n) -> o n", o=1)

        @block.sync
        def _(sp):
            sp.wait_ge(cleared, 9)
            with nc.allow_non_contiguous_dma(reason="a few small weights"):
                sp.dma_start(emb_bias[0:C, :], b_emb.rearrange("(k o) -> k o", o=1)).then_inc(const_loaded, 16)
                sp.dma_start(att_own[0:C, :], W_att[0:C, :]).then_inc(const_loaded, 16)
                sp.dma_start(att_own[C:C + 1, :], b_att.rearrange("(k o) -> k o", o=1)).then_inc(const_loaded, 16)
                sp.dma_start(att_other[0:C, :], W_att[C:2 * C, :]).then_inc(const_loaded, 16)
                sp.dma_start(to_y[0:C, :], W_conv[0:C, :]).then_inc(const_loaded, 16)
                sp.dma_start(to_y[C:C + 1, :], b_conv.rearrange("(o k) -> o k", o=1)).then_inc(const_loaded, 16)
                sp.dma_start(to_y[F0:F0 + C, :], W_conv[C:2 * C, :]).then_inc(const_loaded, 16)

            def load(g, half, i):
                sp.wait_ge(y_made, g * YG + (half + 1) * (YG // 2))
                cols = bass.ds(i * L_COLS + half * 2 * N, L_COLS)
                tiles = bass.ds(i * (L_COLS // P) + half * HALF_TILES, L_COLS // P)
                at = bass.ds(g * COLS + i * L_COLS + half * 2 * N, L_COLS)
                sp.dma_start(points[0:C, cols], unit[:, at]).then_inc(half_loaded[half], 16)
                sp.dma_start(hidden[0:C, cols], feat[:, at]).then_inc(half_loaded[half], 16)
                sp.dma_start(points[C:C + 1, cols], half_sq_row[:, at]).then_inc(half_loaded[half], 16)
                with nc.allow_non_contiguous_dma(reason="a table row for each partition"):
                    sp.dma_start(own[:, tiles, :], table[at, :].rearrange("(k p) c -> p k c", p=P)).then_inc(half_loaded[half], 16)

            def body(g, k, par, pair, batch, y_step, load_step):
                tile = g * TILES + k
                sp.wait_ge(scored, tile * NB + (STAGE_FREE - NB))
                sp.dma_start(queries[0:C, par, :], unit[:, bass.ds(tile * P, P)]).then_inc(staged[par], 16)
                sp.dma_start(queries[C + 1:C + 2, par, :], half_sq_row[:, bass.ds(tile * P, P)]).then_inc(staged[par], 16)
                if load_step is not None:
                    load(*load_step)

            for i in range(L_STEPS):
                load(0, 0, i)
            each_tile(sp, body, lambda g, half: None)

        @block.gpsimd
        def _(pool):
            nc.gpsimd.iota(own_number[:], [[P, TILES]], base=0, channel_multiplier=1).then_inc(numbered, 1)
            pool.wait_ge(cleared, 9)
            nc.gpsimd.affine_select(out=ident[:], in_=ident[:], compare_op=ALU.not_equal, fill=1.0, base=0,
                                    pattern=[[-1, P]], channel_multiplier=1).then_inc(ident_ready, 1)
            with pool.Fori(0, GROUPS * TILES // 2) as i:
                for par in range(2):
                    tile = i * 2 + par
                    pool.wait_ge(near_free, tile + 1)
                    gate(pool, rows_ready, tile + 1, pool_passed)
                    for j in range(1, NEIGHBOURS):
                        pool.indirect_dma_start(near[:, par, j, :], None, table[:, :],
                                                bass.IndirectOffsetOnAxis(ap=row[:, par, j:j + 1], axis=0)).then_inc(near_in[par][j // H8], 16)

        @block.tensor
        def _(pe):
            pe.sem_inc(y_made, YG)
            pe.sem_inc(scored, STAGE_FREE)
            pe.wait_ge(const_loaded, 16 * 7)
            pe.wait_ge(spread_ready, 1)
            nc.tensor.matmul(ps[:, 0:1], spread[:], att_own[:], start=True, stop=False)
            nc.tensor.matmul(ps[:, 0:1], spread[:], att_other[:], start=False, stop=True).then_inc(bias_made, 1)
            pe.wait_ge(const_ready, 1)
            pe.wait_ge(ident_ready, 1)

            def add_doubts(tile):
                gate(pe, doubt_ready, tile + 1, pe_passed)
                gate(pe, sums_in, tile + (SUMS_FREE - TURN_LAG + 1), pe_passed)
                for i in range(2):
                    last = nc.tensor.matmul(ps[0:1, FLAG:FLAG + 1], ones[:], doubt[:, i:i + 1], start=i == 0, stop=i == 1)
                last.then_inc(doubts_made, 1)
                gate(pe, doubts_in, tile + 1, pe_passed)

            def turn(tile, par):
                pe.wait_ge(summed_ready, tile + 1)
                pe.wait_ge(sums_in, tile + SUMS_FREE)
                nc.tensor.transpose(ps[0:C, LAST:LAST + P], summed[:, par, :], ident[:]).then_inc(sums_turned, 1)

            def convolve_1x1(g, half, c):
                at = c * CH + half * 2 * N
                nc.tensor.matmul(ps[0:C, LAST:LAST + CH], to_y[:], hidden[:, bass.ds(at, CH)], start=True, stop=True).then_inc(y_made, 1)

            def body(g, k, par, pair, batch, y_step, load_step):
                tile = g * TILES + k
                if isinstance(k, int) and k in (0, HALF_TILES):
                    gate(pe, half_loaded[k // HALF_TILES], g * (16 * LOADS) + 16 * LOADS, pe_passed)
                pe.wait_ge(staged[par], (g * (TILES // 2) + pair) * 32 + 32)
                parts = [(0, P, batch)] if isinstance(batch, int) else [(0, TAIL, batch[0]), (TAIL, P - TAIL, batch[1])]
                for c, (at, width) in enumerate(BANKS):
                    gate(pe, scores_in, tile * NB + (c + 1), pe_passed)
                    for r0, rows, b in parts:
                        last = nc.tensor.matmul(ps[r0:r0 + rows, at:at + width], queries[:, par, r0:r0 + rows],
                                                points[:, b * N + at:b * N + at + width], start=True, stop=True)
                    last.then_inc(scored, 1)
                    if len(parts) > 1 and c + 1 == EARLY:
                        add_doubts(tile - 1)
                if y_step is not None:
                    y_g, y_half, c = y_step
                    gate(pe, y_in, y_g * YG + c + (y_half * Y_STEPS + Y_FREE), pe_passed)
                if begun(g, k, 1) and len(parts) == 1:
                    add_doubts(tile - 1)
                if begun(g, k, TURN_LAG):
                    turn(tile - TURN_LAG, (par + TURN_LAG) % 2)
                if y_step is not None and not isinstance(c, int):
                    gate(pe, sums_in, tile + (SUMS_FREE - TURN_LAG + 1), pe_passed)
                    convolve_1x1(y_g, y_half, c)

            each_tile(pe, body, lambda g, half: None)
            add_doubts(ALL - 1)
            for tile in range(ALL - TURN_LAG, ALL):
                turn(tile, tile % 2)
            pe.wait_ge(sums_in, ALL + SUMS_FREE)
            for c in range(Y_STEPS):
                pe.wait_ge(y_in, (GROUPS - 1) * YG + Y_STEPS + c + Y_FREE)
                convolve_1x1(GROUPS - 1, 1, c)

        @block.scalar
        def _(act):
            act.sem_inc(scores_in, BANKS_FREE)
            act.sem_inc(sums_in, SUMS_FREE)
            act.sem_inc(y_in, Y_FREE)
            for par in range(2):
                act.sem_inc(y_stored[par], 16)
            act.wait_ge(bias_made, 1)
            nc.scalar.activation(att_bias[:], ps[:, 0:1], ACT.Copy).then_inc(const_ready, 1)

            def copy_doubts(tile):
                act.wait_ge(doubts_made, tile + 1)
                nc.scalar.activation(doubts[:], ps[0:1, FLAG:FLAG + 1], ACT.Copy).then_inc(doubts_in, 1)

            def copy_own(tile, k, par):
                act.wait_ge(near_free, tile + 1)
                nc.scalar.activation(near[:, par, 0:1, :], own[:, bass.ds(k, 1), :], ACT.Copy).then_inc(own_in, 1)

            def exponentiate(tile, par):
                act.wait_ge(logits_ready, tile + 1)
                nc.scalar.activation(expd[:, par, :], logit[:, par, 1, :], ACT.Exp,
                                     accum_out=total[:, par:par + 1]).then_inc(exp_ready, 1)

            def finish(tile, k):
                act.wait_ge(sums_turned, tile + (1 + SUMMED_FREE))
                nc.scalar.activation(hidden[F0:F0 + C, bass.ds(k * P, P)], ps[0:C, LAST:LAST + P],
                                     ACT.Copy).then_inc(sums_in, 1)

            def copy_y(g, half, c):
                for b in range(2):
                    act.wait_ge(y_stored[b], g * 32 + (half + 1) * 16)
                act.wait_ge(y_made, g * YG + c + (half * Y_STEPS + 1 + YG))
                nc.scalar.activation(y_sb[:, bass.ds(c * CH, CH)], ps[0:C, LAST:LAST + CH], ACT.Copy).then_inc(y_in, 1)

            def store_y(g, half):
                for b in range(2):
                    act.wait_ge(y_in, g * YG + ((half + 1) * Y_STEPS + Y_FREE))
                    act.dma_start(y[bass.ds(g * PER + (2 * half + b), 1), :, :].rearrange("o c n -> (o c) n"),
                                  y_sb[:, b * N:(b + 1) * N]).then_inc(y_stored[b], 16)

            def body(g, k, par, pair, batch, y_step, load_step):
                tile = g * TILES + k
                if begun(g, k, EXP_LAG):
                    exponentiate(tile - EXP_LAG, (par + EXP_LAG) % 2)
                act.wait_ge(scores_free, tile + (SCORES_FREE - 1))
                for c, (at, width) in enumerate(BANKS):
                    act.wait_ge(scored, tile * NB + (c + 1 + STAGE_FREE))
                    nc.scalar.activation(scores[:, par, at:at + width], ps[:, at:at + width], ACT.Copy).then_inc(scores_in, 1)
                    if isinstance(batch, tuple) and c + 1 == EARLY:
                        copy_doubts(tile - 1)
                if begun(g, k, 1) and isinstance(batch, int):
                    copy_doubts(tile - 1)
                if begun(g, k, TURN_LAG):
                    finish(tile - TURN_LAG, earlier(k, TURN_LAG))
                if begun(g, k, OWN_LAG):
                    copy_own(tile - OWN_LAG, earlier(k, OWN_LAG), par)
                if y_step is not None and not isinstance(y_step[2], int):
                    copy_y(*y_step)

            def between(g, half):
                if half:
                    store_y(g, 0)
                elif not isinstance(g, int):
                    store_y(g - 1, 1)

            each_tile(act, body, between)
            for lag in range(TURN_LAG, 0, -1):
                exponentiate(ALL - lag, lag % 2)
                if lag == TURN_LAG:
                    copy_doubts(ALL - 1)
                finish(ALL - lag, TILES - lag)
                if lag > OWN_LAG:
                    copy_own(ALL - (lag - OWN_LAG), TILES - (lag - OWN_LAG), lag % 2)
            for c in range(Y_STEPS):
                copy_y(GROUPS - 1, 1, c)
            store_y(GROUPS - 1, 1)
            for b in range(2):
                act.wait_ge(y_stored[b], 16 + 32 * GROUPS)

        @block.vector
        def _(dve):
            dve.sem_inc(scores_free, SCORES_FREE)
            dve.sem_inc(near_free, NEAR_FREE)
            dve.sem_inc(sums_turned, SUMMED_FREE)
            for t, value in ((ident, 0.0), (emb_bias, 1.0), (att_own, 0.0), (att_other, 0.0), (to_y, 0.0)):
                nc.vector.memset(t[:], value).then_inc(cleared, 1)
            nc.vector.memset(spread[:], 1.0).then_inc(chain, 1)
            nc.vector.memset(ones[:], 1.0).then_inc(cleared, 1)
            nc.vector.memset(queries[C:C + 2, :, :], -1.0).then_inc(cleared, 1)
            nc.vector.memset(points[C:C + 2, :], -1.0).then_inc(cleared, 1)
            nc.vector.memset(hidden[C:F0, :], 1.0).then_inc(cleared, 1)
            dve.wait_ge(const_loaded, 16 * 7)
            dve.wait_ge(chain, 1)
            nc.vector.tensor_scalar(spread[:], spread[:], emb_bias[:, 0:1], None, ALU.mult).then_inc(spread_ready, 1)
            dve.sem_clear(chain)
            for k0, k1, rows, b in ((0, FULL + 1, slice(0, P), 0), (FULL, FULL + 1, slice(TAIL, P), 1),
                                    (FULL + 1, HALF_TILES, slice(0, P), 1)):
                for half in range(2):
                    at = half * HALF_TILES
                    if rows.start:
                        dve.wait_ge(chain, 2)
                    nc.vector.memset(batch_row[rows, at + k0:at + k1], float((2 * half + b) * N)).then_inc(chain, 1)
            dve.wait_ge(numbered, 1)
            dve.wait_ge(chain, 6)
            nc.vector.tensor_tensor(own_place[:], own_number[:], batch_row[:], ALU.subtract).then_inc(chain, 1)
            dve.wait_ge(chain, 7)
            dve.sem_clear(chain)
            dve.wait_ge(const_ready, 1)
            steps = [0]

            def step(instruction):
                instruction.then_inc(chain, 1)
                steps[0] += 1
                return steps[0]

            def clear_chain():
                dve.wait_ge(chain, steps[0])
                dve.sem_clear(chain)
                steps[0] = 0

            def rows_placed():
                return step(nc.vector.tensor_copy(placed[:], place[:]))

            def rows_distance(n):
                dve.wait_ge(chain, n)
                return step(nc.vector.tensor_scalar(swap[:], placed[:], -1.0, placed[:, 0:1], ALU.mult, ALU.add))

            def rows_swap(n, k):
                dve.wait_ge(chain, n)
                return step(nc.vector.scalar_tensor_tensor(swap[:], placed[:], own_place[:, bass.ds(k, 1)], swap[:],
                                                           ALU.is_equal, ALU.mult))

            def rows_out(n, k, par):
                dve.wait_ge(chain, n)
                nc.vector.scalar_tensor_tensor(row[:, par, :], placed[:], batch_row[:, bass.ds(k, 1)], swap[:],
                                               ALU.add, ALU.add).then_inc(rows_ready, 1)

            def await_near(par, pair):
                for part, count in zip(near_in[par], (H8 - 1, H8)):
                    gate(dve, part, pair * (16 * count) + 16 * count, dve_passed)

            def logits_raw(tile, k, par):
                dve.wait_ge(own_in, tile + 1)
                return step(nc.vector.tensor_scalar(logit[:, par, 0, :], near[:, par, :, C], own[:, bass.ds(k, 1), C + 1],
                                                    att_bias[:, 0:1], ALU.add, ALU.add))

            def logits_leaky(n, par):
                raw = logit[:, par, 0, :]
                dve.wait_ge(chain, n)
                return step(nc.vector.scalar_tensor_tensor(raw, raw, 0.1, raw, ALU.mult, ALU.max))

            def logits_top(n, par):
                dve.wait_ge(chain, n)
                return step(nc.vector.reduce_max(top[:], logit[:, par, 0, :], AX.X))

            def logits_out(n, par):
                dve.wait_ge(chain, n)
                nc.vector.tensor_scalar(logit[:, par, 1, :], logit[:, par, 0, :], top[:, 0:1], None,
                                        ALU.subtract).then_inc(logits_ready, 1)

            def sums_inverse(tile, par):
                dve.wait_ge(exp_ready, tile + 1)
                return step(nc.vector.reciprocal(inverse[:], total[:, par:par + 1]))

            def sums_attention(n, par):
                dve.wait_ge(chain, n)
                return step(nc.vector.tensor_scalar(attn[:], expd[:, par, :], inverse[:, 0:1], None, ALU.mult))

            def sums_weighted(n, par):
                dve.wait_ge(chain, n)
                return step(nc.vector.tensor_tensor(weighted[:], near[:, par, :, 0:C],
                                                    attn[:].rearrange("p (k o) -> p k o", o=1).to_broadcast([P, NEIGHBOURS, C]), ALU.mult))

            def sums_out(n, tile, par):
                dve.wait_ge(chain, n)
                dve.sem_inc(near_free, 1)
                dve.wait_ge(sums_turned, tile + (SUMMED_FREE - 1))
                nc.vector.tensor_reduce(summed[:, par, :], weighted[:].rearrange("p k c -> p c k"), AX.X, ALU.add).then_inc(summed_ready, 1)

            def body(g, k, par, pair, batch, y_step, load_step):
                tile = g * TILES + k
                rows_due, attention_due = begun(g, k, ROW_LAG), begun(g, k, ATT_LAG)
                row_k, att_k, other = earlier(k, ROW_LAG), earlier(k, ATT_LAG), 1 - par
                att_tile = tile - ATT_LAG
                s = scores[:, par, :]

                def search(*parts):
                    for c in parts:
                        n = step(nc.vector.max(found[:, c, :], s[:, c * PART:(c + 1) * PART]))
                    return n

                gate(dve, scores_in, tile * NB + (EARLY + BANKS_FREE), dve_passed)
                search(0)
                if rows_due:
                    n = rows_placed()
                search(1)
                if rows_due:
                    n = rows_distance(n)
                search(2)
                if rows_due:
                    n = rows_swap(n, row_k)
                search(3)
                if attention_due:
                    await_near(other, g * (TILES // 2) + pair - 2 + par)
                if rows_due:
                    rows_out(n, row_k, other)
                search(4)
                if attention_due:
                    n = logits_raw(att_tile, att_k, other)
                search(5)
                if attention_due:
                    n = logits_leaky(n, other)
                search(6)
                if attention_due:
                    n = logits_top(n, other)
                search(7)
                if attention_due:
                    logits_out(n, other)
                search(8)
                gate(dve, scores_in, tile * NB + (NB + BANKS_FREE), dve_passed)
                search(9, 10)
                if attention_due:
                    n = sums_inverse(att_tile, other)
                search(11)
                if attention_due:
                    n = sums_attention(n, other)
                all_found = search(12, 13)
                if attention_due:
                    n = sums_weighted(n, other)
                found_all = found[:].rearrange("p a b -> p (a b)")
                dve.wait_ge(chain, all_found)
                eight = step(nc.vector.max(best[:, 0:H8], found_all))
                if attention_due:
                    sums_out(n, att_tile, other)
                dve.wait_ge(chain, eight)
                n = step(nc.vector.match_replace(rest[:], best[:, 0:H8], found_all, NEVER))
                step(nc.vector.reduce_max(best[:, PASSED:PASSED + 1], found[:, :, H8 - 1], AX.X))
                dve.wait_ge(chain, n)
                n = step(nc.vector.max(best[:, H8:NEIGHBOURS], rest[:]))
                dve.wait_ge(chain, n)
                nc.vector.tensor_tensor(doubt[:], best[:, H8::H8], best[:, H8 - 1:NEIGHBOURS:H8], ALU.is_ge).then_inc(doubt_ready, 1)
                step(nc.vector.max_index(place[:, 0:H8], best[:, 0:H8], s))
                before = steps[0]
                gate(dve, doubts_in, tile + 1, dve_passed)
                in_doubt = dve.value_load(doubts[0:1, 0:1], min_val=0, max_val=2 * P)
                dve.wait_ge(chain, before)
                with dve.If(in_doubt > 0):
                    nc.vector.match_replace(s, best[:, 0:H8], s, NEVER).then_inc(chain, 1)
                    dve.wait_ge(chain, before + 1)
                    nc.vector.max(best[:, H8:NEIGHBOURS], s).then_inc(chain, 1)
                    dve.wait_ge(chain, before + 2)
                    nc.vector.max_index(place[:, H8:], best[:, H8:NEIGHBOURS], s).then_inc(chain, 1)
                with dve.Else():
                    nc.vector.max_index(place[:, H8:], best[:, H8:NEIGHBOURS], s).then_inc(chain, 3)
                steps[0] += 3
                dve.wait_ge(chain, steps[0])
                dve.sem_inc(scores_free, 1)
                clear_chain()
                if isinstance(k, int) and k == 0 and not isinstance(g, int):
                    dve.wait_ge(rows_ready, g * TILES)
                    step(nc.vector.tensor_scalar(batch_row[:], batch_row[:], float(PER * N), None, ALU.add))
                    clear_chain()

            each_tile(dve, body, lambda g, half: None)
            n = rows_swap(rows_distance(rows_placed()), TILES - 1)
            for tile in range(ALL - ATT_LAG, ALL):
                k, par = tile - ALL + TILES, tile % 2
                await_near(par, tile // 2)
                if tile == ALL - ATT_LAG:
                    rows_out(n, TILES - 1, 1)
                logits_out(logits_top(logits_leaky(logits_raw(tile, k, par), par), par), par)
                n = sums_attention(sums_inverse(tile, par), par)
                sums_out(sums_weighted(n, par), tile, par)


def normalise_output(nc, y, base, gamma, beta, out):
    y_rows = y.rearrange("b c n -> (b c) n")
    base_rows = base.rearrange("b c n -> (b c) n")
    out_rows = out.rearrange("b c h w -> (b c) (h w)")
    with ExitStack() as stack:
        enter = stack.enter_context
        y_all = enter(nc.sbuf_tensor("y_all", [P, GROUPS, N], FP32))
        base_sb = enter(nc.sbuf_tensor("base_sb", [P, 4, N], FP32))
        stats = enter(nc.sbuf_tensor("stats_o", [P, GROUPS * NCH, 6], FP32))
        moments = enter(nc.sbuf_tensor("moments_o", [P, 2], FP32))
        small = enter(nc.sbuf_tensor("small_o", [P, 8], FP32))
        affine = enter(nc.sbuf_tensor("affine", [P, 2], FP32))
        average = enter(nc.sbuf_tensor("average", [P, P], FP32))
        average_ps = enter(nc.psum_tensor("average_ps", [P, 2], FP32))
        cleared = enter(nc.semaphore("o_cleared"))
        const_loaded = enter(nc.semaphore("o_const"))
        average_ready = enter(nc.semaphore("o_average"))
        chain = enter(nc.semaphore("o_chain"))
        averaged = enter(nc.semaphore("o_averaged"))
        std_ready = enter(nc.semaphore("o_std"))
        coef_ready = enter(nc.semaphore("o_coef"))
        relu_ready = enter(nc.semaphore("o_relu"))
        added = enter(nc.semaphore("o_added"))
        y_loaded = [enter(nc.semaphore(f"o_y{g}")) for g in range(GROUPS)]
        base_loaded = [enter(nc.semaphore(f"o_b{g}")) for g in range(GROUPS)]
        stored = [enter(nc.semaphore(f"o_s{g}")) for g in range(GROUPS)]
        block = enter(nc.Block())
        mean, second, dev, std, scale, shift, eps, var = range(8)

        def col(i):
            return small[:, i:i + 1]

        @block.sync
        def _(sp):
            for b in range(PER):
                for i, src in enumerate((gamma, beta)):
                    sp.dma_start(affine[C * b:C * (b + 1), i:i + 1], src.rearrange("(c o) -> c o", o=1)).then_inc(const_loaded, 16)
            for g in range(GROUPS):
                sp.dma_start(y_all[:, g, :], y_rows[g * P:(g + 1) * P, :]).then_inc(y_loaded[g], 16)
            for g in range(GROUPS):
                if g >= 4:
                    sp.wait_ge(stored[g - 4], 16)
                sp.dma_start(base_sb[:, g % 4, :], base_rows[g * P:(g + 1) * P, :]).then_inc(base_loaded[g], 16)

        @block.gpsimd
        def _(pool):
            nc.gpsimd.memset(average[:], 0.0).then_inc(average_ready, 1)
            for n, d in enumerate(range(1 - PER, PER)):
                pool.wait_ge(average_ready, n + 1)
                nc.gpsimd.affine_select(out=average[:], in_=average[:], compare_op=ALU.not_equal, fill=1.0 / PER,
                                        base=C * d, pattern=[[-1, P]], channel_multiplier=1).then_inc(average_ready, 1)
            for g in range(GROUPS):
                pool.wait_ge(added, g + 1)
                pool.dma_start(out_rows[g * P:(g + 1) * P, :], y_all[:, g, :]).then_inc(stored[g], 16)
            for g in range(GROUPS):
                pool.wait_ge(stored[g], 16)

        @block.vector
        def _(dve):
            steps = [0]

            def link(instruction):
                steps[0] += 1
                instruction.then_inc(chain, 1)
                dve.wait_ge(chain, steps[0])

            link(nc.vector.memset(col(eps), EPS))
            for g in range(GROUPS):
                dve.wait_ge(y_loaded[g], 16)
                for c in range(NCH):
                    nc.vector.bn_stats(stats[:, g * NCH + c, :], y_all[:, g, c * CH:(c + 1) * CH]).then_inc(chain, 1)
                    steps[0] += 1
            dve.wait_ge(chain, steps[0])
            link(nc.vector.bn_aggr(moments[:], stats[:].rearrange("p a b -> p (a b)")))
            dve.sem_inc(cleared, 1)
            dve.wait_ge(averaged, 1)
            link(nc.vector.tensor_copy(col(mean), average_ps[:, 0:1]))
            link(nc.vector.tensor_tensor(col(dev), moments[:, 0:1], col(mean), ALU.subtract))
            link(nc.vector.tensor_tensor(col(second), col(dev), col(dev), ALU.mult))
            link(nc.vector.tensor_tensor(col(second), col(second), moments[:, 1:2], ALU.add))
            dve.sem_inc(cleared, 1)
            dve.wait_ge(averaged, 2)
            link(nc.vector.tensor_copy(col(var), average_ps[:, 1:2]))
            dve.sem_inc(cleared, 1)
            dve.wait_ge(std_ready, 1)
            link(nc.vector.reciprocal(col(scale), col(std)))
            dve.wait_ge(const_loaded, 16 * 2 * PER)
            link(nc.vector.tensor_tensor(col(scale), col(scale), affine[:, 0:1], ALU.mult))
            link(nc.vector.tensor_tensor(col(shift), col(scale), col(mean), ALU.mult))
            link(nc.vector.tensor_tensor(col(shift), affine[:, 1:2], col(shift), ALU.subtract))
            dve.sem_inc(coef_ready, 1)
            for g in range(GROUPS):
                dve.wait_ge(relu_ready, g + 1)
                dve.wait_ge(base_loaded[g], 16)
                nc.vector.tensor_tensor(y_all[:, g, :], y_all[:, g, :], base_sb[:, g % 4, :], ALU.add).then_inc(added, 1)

        @block.tensor
        def _(pe):
            pe.wait_ge(average_ready, 2 * PER)
            pe.wait_ge(cleared, 1)
            nc.tensor.matmul(average_ps[:, 0:1], average[:], moments[:, 0:1], start=True, stop=True).then_inc(averaged, 1)
            pe.wait_ge(cleared, 2)
            nc.tensor.matmul(average_ps[:, 1:2], average[:], col(second), start=True, stop=True).then_inc(averaged, 1)

        @block.scalar
        def _(act):
            act.wait_ge(cleared, 3)
            nc.scalar.activation(col(std), col(var), ACT.Sqrt, bias=col(eps)).then_inc(std_ready, 1)
            act.wait_ge(coef_ready, 1)
            for g in range(GROUPS):
                nc.scalar.activation(y_all[:, g, :], y_all[:, g, :], ACT.Relu, bias=col(shift), scale=col(scale)).then_inc(relu_ready, 1)


def build(nc, x, weight, bias, W_emb, b_emb, W_att, b_att, W_conv, b_conv, gamma, beta, out):
    xg = nc.dram_tensor("xg", [C, HP, BATCH, WP], FP32).ap()
    conv, base, y = (nc.dram_tensor(name, [BATCH, C, N], FP32).ap() for name in ("conv", "base", "y"))
    feat, unit = (nc.dram_tensor(name, [C, BATCH * N], FP32).ap() for name in ("feat", "unit"))
    half_sq = nc.dram_tensor("half_sq", [BATCH * N], FP32).ap()
    table = nc.dram_tensor("table", [BATCH * N, ROWLEN], FP32).ap()
    normalise_input(nc, x, xg)
    convolve(nc, weight, xg, conv)
    prepare(nc, x, conv, bias, W_emb, W_att, feat, unit, base, half_sq, table)
    attend(nc, feat, unit, half_sq, table, W_emb, b_emb, W_att, b_att, W_conv, b_conv, y)
    normalise_output(nc, y, base, gamma, beta, out)


_INS = ["x", "L0_conv_weight", "L0_conv_bias", "L1_conv_W_emb", "L1_conv_b_emb", "L1_conv_W_att", "L1_conv_b_att",
        "L1_conv_W_conv", "L1_conv_b_conv", "L1_conv_gamma", "L1_conv_beta"]
_OUTS = [((BATCH, C, H, W), "float32")]


def kernel(**inputs):
    import numpy as _np
    import concourse.bacc as _bacc
    from concourse import mybir as _mybir
    from concourse.bass_utils import run_bass_kernel_spmd as _run

    nc = _bacc.Bacc("TRN2", target_bir_lowering=False, num_devices=1)
    arrays, args = {}, []
    for name in _INS:
        a = _np.ascontiguousarray(inputs[name])
        arrays[f"in_{name}_dram"] = a
        args.append(nc.dram_tensor(f"in_{name}_dram", a.shape, _mybir.dt.from_np(a.dtype), kind="ExternalInput").ap())
    for i, (shape, dtype) in enumerate(_OUTS):
        dt = _mybir.dt.from_np(_np.dtype(dtype))
        args.append(nc.dram_tensor(f"out_{i}_dram", shape, dt, kind="ExternalOutput").ap())
    build(nc, *args)
    r = _run(nc, [arrays], core_ids=[0])
    return r.results[0]["out_0_dram"]
```
